# Optimizing a Trainium2 kernel written in Bass

```python
import numpy as np
import jax
import jax.numpy as jnp

def _softmax(x, axis=-1):
    return jax.nn.softmax(x, axis=axis)

def _gelu(x):
    return jax.nn.gelu(x, approximate=True)

def _silu(x):
    return jax.nn.silu(x)

def _sigmoid(x):
    return jax.nn.sigmoid(x)

def _layernorm(x, axis=-1, eps=1e-05):
    m = jnp.mean(x, axis=axis, keepdims=True)
    v = jnp.var(x, axis=axis, keepdims=True)
    return (x - m) / jnp.sqrt(v + eps)

def _scatter_add(tgt, idx, src, axis=0):
    return tgt.at[idx].add(src)

def _segment_sum(src, seg, n):
    return jax.ops.segment_sum(src, seg, n)
kernel_name = 'mk_gnn_resnorm_d1_gnn_r8_327bd9'

def setup_inputs(seed: int=0):
    np.random.seed(seed)
    _w = jnp.asarray

    def _rec_inputs():
        import jax
        import jax.numpy as jnp
        _gk = jax.random.key(seed)
        x = -0.000202 + 1 * jax.random.normal(jax.random.fold_in(_gk, 1), (12500, 128), jnp.float32)
        src = jax.random.randint(jax.random.fold_in(_gk, 2), (200000,), 0, 12500, jnp.int32)
        dst = jax.random.randint(jax.random.fold_in(_gk, 3), (200000,), 0, 12500, jnp.int32)
        _o = jnp.argsort(dst, stable=True)
        src = src[_o]
        dst = dst[_o]
        edge_attr_128 = -5.16925e-05 + 1.00005 * jax.random.normal(jax.random.fold_in(_gk, 11), (200000, 128), jnp.float32)
        return (x, src, dst, edge_attr_128)
    x, src, dst, edge_attr_128 = _rec_inputs()

    def _L0_gnn_setup():
        import jax, jax.numpy as jnp
        import numpy as np
        N, E, D, H = (6250, 100000, 128, 8)
        C = D // H
        NEG_SLOPE = 0.2
        EPS = 1e-05

        def _layer_norm(x, w):
            mu = x.mean(-1, keepdims=True)
            var = ((x - mu) ** 2).mean(-1, keepdims=True)
            return (x - mu) / jnp.sqrt(var + EPS) * w
        key = jax.random.key(seed)
        ks = jax.random.split(key, 9)
        s = 0.05
        return {'x': jax.random.normal(ks[0], (N, D), dtype=jnp.float32), 'edge_index': jax.random.randint(ks[1], (2, E), 0, N, dtype=jnp.int32), 'edge_attr': jax.random.normal(ks[2], (E, D), dtype=jnp.float32), 'ln1_w': jnp.ones((D,), jnp.float32), 'lin_l_w': jax.random.normal(ks[3], (D, D), dtype=jnp.float32) * s, 'lin_l_b': jnp.zeros((D,), jnp.float32), 'lin_r_w': jax.random.normal(ks[4], (D, D), dtype=jnp.float32) * s, 'lin_r_b': jnp.zeros((D,), jnp.float32), 'lin_edge_w': jax.random.normal(ks[5], (D, D), dtype=jnp.float32) * s, 'att': jax.random.normal(ks[6], (H, C), dtype=jnp.float32) * s, 'attn_bias': jnp.zeros((D,), jnp.float32), 'ln2_w': jnp.ones((D,), jnp.float32), 'fc_w': jax.random.normal(ks[7], (4 * D, D), dtype=jnp.float32) * s, 'proj_w': jax.random.normal(ks[8], (D, 4 * D), dtype=jnp.float32) * s}
    _L0_gnn_all = _L0_gnn_setup()
    _L0_gnn_in = {k: v for k, v in _L0_gnn_all.items() if k in ('ln1_w', 'lin_l_w', 'lin_l_b', 'lin_r_w', 'lin_r_b', 'lin_edge_w', 'att', 'attn_bias', 'ln2_w', 'fc_w', 'proj_w')}
    del _L0_gnn_all
    return {'x': x, 'src': src, 'dst': dst, 'edge_attr_128': edge_attr_128, 'L0_gnn_ln1_w': _L0_gnn_in['ln1_w'], 'L0_gnn_lin_l_w': _L0_gnn_in['lin_l_w'], 'L0_gnn_lin_l_b': _L0_gnn_in['lin_l_b'], 'L0_gnn_lin_r_w': _L0_gnn_in['lin_r_w'], 'L0_gnn_lin_r_b': _L0_gnn_in['lin_r_b'], 'L0_gnn_lin_edge_w': _L0_gnn_in['lin_edge_w'], 'L0_gnn_att': _L0_gnn_in['att'], 'L0_gnn_attn_bias': _L0_gnn_in['attn_bias'], 'L0_gnn_ln2_w': _L0_gnn_in['ln2_w'], 'L0_gnn_fc_w': _L0_gnn_in['fc_w'], 'L0_gnn_proj_w': _L0_gnn_in['proj_w']}

def reference(x, src, dst, edge_attr_128, L0_gnn_ln1_w, L0_gnn_lin_l_w, L0_gnn_lin_l_b, L0_gnn_lin_r_w, L0_gnn_lin_r_b, L0_gnn_lin_edge_w, L0_gnn_att, L0_gnn_attn_bias, L0_gnn_ln2_w, L0_gnn_fc_w, L0_gnn_proj_w):
    import jax
    import jax.numpy as jnp

    def _L0_gnn_ref(x, edge_index, edge_attr, ln1_w, lin_l_w, lin_l_b, lin_r_w, lin_r_b, lin_edge_w, att, attn_bias, ln2_w, fc_w, proj_w):
        import jax, jax.numpy as jnp
        import numpy as np
        N, E, D, H = (6250, 100000, 128, 8)
        C = D // H
        NEG_SLOPE = 0.2
        EPS = 1e-05

        def _layer_norm(x, w):
            mu = x.mean(-1, keepdims=True)
            var = ((x - mu) ** 2).mean(-1, keepdims=True)
            return (x - mu) / jnp.sqrt(var + EPS) * w
        n, d = x.shape
        h_heads, c = att.shape
        h = _layer_norm(x, ln1_w)
        xl = (h @ lin_l_w.T + lin_l_b).reshape(n, h_heads, c)
        xr = (h @ lin_r_w.T + lin_r_b).reshape(n, h_heads, c)
        e = (edge_attr @ lin_edge_w.T).reshape(-1, h_heads, c)
        src, dst = (edge_index[0], edge_index[1])
        z = jax.nn.leaky_relu(xl[src] + xr[dst] + e, NEG_SLOPE)
        logits = jnp.einsum('ehc,hc->eh', z, att)
        m = jax.lax.stop_gradient(jax.ops.segment_max(logits, dst, num_segments=n))
        num = jnp.exp(logits - m[dst])
        den = jax.ops.segment_sum(num, dst, num_segments=n)
        alpha = num / den[dst]
        msg = xl[src] * alpha[..., None]
        attn_out = jax.ops.segment_sum(msg, dst, num_segments=n).reshape(n, d) + attn_bias
        x = x + attn_out
        h2 = _layer_norm(x, ln2_w)
        x = x + jax.nn.relu(h2 @ fc_w.T) @ proj_w.T
        return x
    edge_index = jnp.stack([src, dst])
    x = _layernorm(x + _L0_gnn_ref(x, edge_index, edge_attr_128, L0_gnn_ln1_w, L0_gnn_lin_l_w, L0_gnn_lin_l_b, L0_gnn_lin_r_w, L0_gnn_lin_r_b, L0_gnn_lin_edge_w, L0_gnn_att, L0_gnn_attn_bias, L0_gnn_ln2_w, L0_gnn_fc_w, L0_gnn_proj_w), axis=-1)
    return x

_drawn_inputs = setup_inputs


def setup_inputs(seed=0):
    import zlib

    import numpy as np

    out = dict(_drawn_inputs(seed))
    spreads = {'L0_gnn_ln1_w': (1.0, 0.6),
     'L0_gnn_lin_l_b': (0.0, 0.1),
     'L0_gnn_lin_r_b': (0.0, 2.0),
     'L0_gnn_attn_bias': (0.0, 0.1),
     'L0_gnn_ln2_w': (1.0, 0.2)}
    factors = {'edge_attr_128': 8.0, 'L0_gnn_lin_r_w': 8.0, 'L0_gnn_lin_edge_w': 8.0, 'L0_gnn_att': 5.197}
    for name, (base, spread) in spreads.items():
        noise = np.random.default_rng([zlib.crc32(name.encode()), seed]).standard_normal(out[name].shape)
        drawn = base * np.exp(spread * noise) if base else spread * noise
        out[name] = jnp.asarray(drawn.astype(out[name].dtype))
    for name, factor in factors.items():
        out[name] = (out[name] * factor).astype(out[name].dtype)
    return out
```

```python
from contextlib import ExitStack

import concourse.bass as bass
from concourse import mybir

P = 128
N, E, D, H = 12500, 200000, 128, 8
HC = D // H
CH = 15
EG = CH * P
G = -(-E // EG)
EP = G * EG
CW = CH + 1
GROUPS = [(0, 4), (4, 4), (8, 4), (12, 3)]
UN = 3
NB = 4
BATCHES = 26
NP = BATCHES * NB * P
WT = 208
HID = 4 * D
MAX_ROUNDS = -(-(G + N // P) // UN)
MS = HC + 1
AW = H * MS
BIG = 1.0e30
EPS = 1e-05
SLOPE = 0.2
assert G <= P and G % UN == 0 and G // UN > 2 and NP >= N + P and MAX_ROUNDS * UN < WT

ALU = mybir.AluOpType
ACT = mybir.ActivationFunctionType
AX = mybir.AxisListType
F32 = mybir.dt.float32
BF16 = mybir.dt.bfloat16
I32 = mybir.dt.int32


def gnn_kernel(nc, x, ea_t, edges, dst_row, bounds, ln1_w, wlr_t, blr, we_t, att, attn_bias,
               ln2_w, fc_t, proj_t, out):
    xl_tab = nc.dram_tensor("xl_tab", (NP, D), F32, kind="Internal").ap()
    xr_tab = nc.dram_tensor("xr_tab", (NP, 3, D), BF16, kind="Internal").ap()

    with ExitStack() as ctx:
        def sb(name, shape, dt=F32):
            return ctx.enter_context(nc.sbuf_tensor(name, shape, dt))

        def ps(name, shape, dt=F32):
            return ctx.enter_context(nc.psum_tensor(name, shape, dt))

        def sem(name):
            return ctx.enter_context(nc.semaphore(name))

        def sems(name, n):
            return [sem(f"{name}{k}") for k in range(n)]

        ident = sb("ident", [P, P])
        ident16 = sb("ident16", [P, P], BF16)
        ones = sb("ones", [P, P])
        tri = sb("tri", [P, P])
        iota_p = sb("iota_p", [P, 1])
        iota_w = sb("iota_w", [P, WT])
        node_no = sb("node_no", [P, P, CW], BF16)
        w_lr = sb("w_lr", [P, 2 * D])
        b_lr = sb("b_lr", [P, 2 * D])
        w_e = sb("w_e", [P, D])
        w_fc = sb("w_fc", [P, HID])
        w_pr = sb("w_pr", [P, 4, D])
        att_b = sb("att_b", [P, D])
        a_bias = sb("a_bias", [P, D])
        ln1 = sb("ln1", [P, 1])
        ln2 = sb("ln2", [P, 1])
        bnd = sb("bnd", [P, 2], I32)
        bnd_d = sb("bnd_d", [P, 1], I32)
        bnd_f = sb("bnd_f", [P, 8])
        tabs = sb("tabs", [P, 4, WT])
        base_f = sb("base_f", [P, WT])
        delta_f = sb("delta_f", [P, WT])
        item_i = sb("item_i", [P, 2, WT], I32)
        cnt_f = sb("cnt_f", [P, 2, P])
        more_i = sb("more_i", [P, 1], I32)
        px = sb("px", [P, 2, NB, D])
        pst = sb("pst", [P, 2, NB, 6])
        pmv = sb("pmv", [P, 2, NB, 2])
        prs = sb("prs", [P, 2, NB])
        plv = sb("plv", [P, 2, NB])
        eps_t = sb("eps_t", [P, 1])
        phn = sb("phn", [P, 2, NB, D])
        pht = sb("pht", [P, 2, NB * P])
        pf = sb("pf", [P, 2, NB, 2 * D])
        pres = sb("pres", [P, 2, NB, D])
        pxr = sb("pxr", [P, 2, NB, 3, D], BF16)
        edg = sb("edg", [P, UN, 3, CW], I32)
        drow = sb("drow", [P, UN, P], I32)
        ea = sb("ea", [P, UN, EG])
        gx = sb("gx", [P, UN, CH, D])
        xrw = sb("xrw", [P, UN, 3, D], BF16)
        xw = sb("xw", [P, UN, D])
        dl = sb("dl", [P, UN, CW], BF16)
        runf = sb("runf", [P, UN, P])
        m16 = sb("m16", [P, UN, P, CW], BF16)
        m32 = sb("m32", [P, UN, CH, P])
        mt = sb("mt", [P, UN, CH * P], BF16)
        zr = sb("zr", [P, CH, D])
        zl = sb("zl", [P, CH, D])
        lg = sb("lg", [P, UN, CH * H])
        scan = sb("scan", [P, P])
        vlast = sb("vlast", [P, CH, H])
        vs = sb("vs", [P, UN, CH, 2 * H + 1], BF16)
        pen = sb("pen", [P, CH])
        cand = sb("cand", [P, CH, H])
        mblk = sb("mblk", [P, H])
        pen2 = sb("pen2", [P, 1])
        ms = sb("ms", [P, 2 * H], BF16)
        farg = sb("farg", [P, H])
        fac = sb("fac", [P, UN, H])
        dlt = sb("dlt", [P, CH * H])
        dmin = sb("dmin", [P, CH * H])
        msg = sb("msg", [P, CH * H, MS])
        accs = sb("accs", [P, UN, AW + H + 1])
        tmpa = sb("tmpa", [P, AW])
        sel = sb("sel", [P, UN, P])
        rden = sb("rden", [P, 2, H])
        attn = sb("attn", [P, D])
        xab = sb("xab", [P, D])
        x1 = sb("x1", [P, UN, D])
        y1 = sb("y1", [P, UN, D])
        st2 = sb("st2", [P, 2, 6])
        mv2 = sb("mv2", [P, 2, 2])
        ln_v = sb("ln_v", [P, 2])
        rs2 = sb("rs2", [P, 2])
        hn = sb("hn", [P, D])
        hnt = sb("hnt", [P, P])
        hid = sb("hid", [P, 4, P])
        ob = sb("ob", [P, UN, D])

        pz = ps("pz", [P, 3, 4, D])
        pmt = ps("pmt", [P, 2, 8 * P], BF16)
        pch = ps("pch", [P, 512])
        pag = ps("pag", [P, 512])
        pnd = ps("pnd", [P, 512])
        ch_lt, ch_vt, ch_cand, ch_sh = pch[:, 0:P], pch[:, P:P + CH * H], pch[:, 248:248 + 9 * CH], pch[:, 384:384 + CH * H]
        carry, aggr = pag[:, 0:AW + H + 1], pag[:, 256:256 + AW]

        w_loaded = sem("w_loaded")
        consts = sem("consts")
        scaled = sem("scaled")
        scaled_t = sem("table_steps")
        tables = sem("tables")
        tab_ps = sem("tab_ps")
        ptab = sem("ptab")
        px_loaded = sems("px_loaded", 2)
        p_stats = sem("p_stats")
        p_bn = sem("p_bn")
        p_rstd = sem("p_rstd")
        p_ln = sem("p_ln")
        p_hn = sem("p_hn")
        p_tr = sem("p_tr")
        p_ht = sem("p_ht")
        p_mm = sem("p_mm")
        p_add = sem("p_add")
        p_hi = sem("p_hi")
        p_res = sem("p_res")
        p_mid = sem("p_mid")
        p_low = sem("p_low")
        p_stored = sems("p_stored", 2)
        idx_loaded = sems("idx_loaded", UN)
        ea_loaded = sems("ea_loaded", UN)
        xw_loaded = sems("xw_loaded", UN)
        gathered = sems("gathered", UN)
        stored = sem("stored")
        pe_lt = sem("pe_lt"); pe_z = sem("pe_z"); pe_mt = sem("pe_mt"); pe_carry = sem("pe_carry")
        pe_vt = sem("pe_vt"); pe_sel = sem("pe_sel"); pe_sh = sem("pe_sh"); pe_ht = sem("pe_ht")
        pe_fc = sem("pe_fc"); pe_agg = sem("pe_agg"); pe_proj = sem("pe_proj")
        a_runf = sem("a_runf"); a_mt = sem("a_mt"); a_hi = sem("a_hi"); a_relu = sem("a_relu")
        a_ln = sem("a_ln"); a_rs = sem("a_rs"); a_m32 = sem("a_m32"); a_hnt = sem("a_hnt")
        a_hid = sem("a_hid"); a_fac = sem("a_fac"); a_exp = sem("a_exp")
        v_dl = sem("v_dl"); v_last = sem("v_last"); v_diff = sem("v_diff"); v_m = sem("v_m")
        v_scan = sem("v_scan"); v_tmp = sem("v_tmp"); v_acc = sem("v_acc"); v_vlast = sem("v_vlast")
        v_low = sem("v_low"); v_leak = sem("v_leak"); v_att = sem("v_att"); v_lg = sem("v_lg")
        v_pen = sem("v_pen"); v_cand = sem("v_cand"); v_mblk = sem("v_mblk"); v_max = sem("v_max")
        v_farg = sem("v_farg"); v_mhi = sem("v_mhi"); v_mlo = sem("v_mlo"); v_dlt = sem("v_dlt")
        v_dmin = sem("v_dmin"); v_msg = sem("v_msg"); v_den = sem("v_den"); v_rden = sem("v_rden")
        v_attn = sem("v_attn"); v_xab = sem("v_xab"); v_x1 = sem("v_x1"); v_st = sem("v_st")
        v_mv = sem("v_mv"); v_hn = sem("v_hn"); v_y1 = sem("v_y1")
        v_y = sem("v_y"); v_stf = sem("v_stf"); v_mvf = sem("v_mvf")
        v_out = sem("v_out"); v_pen2 = sem("v_pen2"); v_sel = sem("v_sel")

        LOADS = 10
        PEEL = 2 * UN

        def items(eng, body, depth):
            eng.wait_ge(tables, 1)
            more = eng.value_load(more_i[0:1, 0:1], min_val=0, max_val=MAX_ROUNDS - G // UN)
            n_rounds = eng.snap(more + G // UN)
            n_items = eng.snap(n_rounds * UN)
            for w in range(PEEL):
                body(w, w % UN, w // UN, 0, min(depth, w + 1))
            with eng.Fori(PEEL // UN, n_rounds) as r:
                w0 = eng.snap(r * UN)
                for j in range(UN):
                    body(w0 + j, j, r, 0, depth)
            for j in range(depth - 1):
                body(n_items + j, j % UN, n_rounds + j // UN, j + 1, depth)
            return n_items

        def done(w, back, n=1, per=1):
            return w * per + (n - back * per)

        def in_slot(r, j, back, per):
            return r * per + ((j - back) // UN + 1) * per

        sp_passed, pool_passed, dve_passed = sem("sp_passed"), sem("pool_passed"), sem("dve_passed")

        def alone(eng, passed):
            eng.sem_inc(passed, 1)

        block = ctx.enter_context(nc.Block())

        @block.sync
        def _(sp):
            sp.dma_start(bnd[:], bounds).then_inc(w_loaded, 16)
            sp.dma_start(w_lr[:], wlr_t).then_inc(w_loaded, 16)
            sp.dma_start(b_lr[:], blr.broadcast_to([P, 2 * D])).then_inc(w_loaded, 16)
            sp.dma_start(ln1[:], ln1_w).then_inc(w_loaded, 16)
            sp.dma_start(ln2[:], ln2_w).then_inc(w_loaded, 16)
            sp.dma_start(w_e[:], we_t).then_inc(w_loaded, 16)
            sp.dma_start(w_fc[:], fc_t).then_inc(w_loaded, 16)
            sp.dma_start(w_pr[:], proj_t).then_inc(w_loaded, 16)
            sp.dma_start(att_b[:], att.broadcast_to([P, D])).then_inc(w_loaded, 16)
            sp.dma_start(a_bias[:], attn_bias.broadcast_to([P, D])).then_inc(w_loaded, 16)

            xb = x.rearrange("(t s p j) d -> t s p j d", s=2, p=P, j=NB)
            xlb = xl_tab.rearrange("(t s p j) d -> t s p j d", s=2, p=P, j=NB)
            xrb = xr_tab.rearrange("(t s p j) k d -> t s p j k d", s=2, p=P, j=NB)

            def p_load(t, s):
                sp.dma_start(px[:, s], xb[bass.ds(t, 1), s].rearrange("a p j d -> (a p) j d")).then_inc(px_loaded[s], 16)

            def p_store(t, s):
                sp.wait_ge(p_add, 4 * t + (2 * s + 2))
                alone(sp, sp_passed)
                sp.dma_start(xlb[bass.ds(t, 1), s].rearrange("a p j d -> (a p) j d"),
                             pf[:, s, :, 0:D]).then_inc(p_stored[s], 16)
                sp.wait_ge(p_low, 2 * t + (s + 1))
                alone(sp, sp_passed)
                sp.dma_start(xrb[bass.ds(t, 1), s].rearrange("a p j k d -> (a p) j k d"),
                             pxr[:, s]).then_inc(p_stored[s], 16)

            p_load(0, 0)
            p_load(0, 1)
            with sp.Fori(0, BATCHES // 2 - 1) as t:
                for s in range(2):
                    sp.wait_ge(p_hn, 2 * t + (s + 1))
                    alone(sp, sp_passed)
                    p_load(t + 1, s)
                    p_store(t, s)
            for s in range(2):
                p_store(BATCHES // 2 - 1, s)
            for s in range(2):
                sp.wait_ge(p_stored[s], 16 * BATCHES)

            def step(w, j, r, lo, hi):
                if lo <= 5 < hi:
                    s = (j - 5) % UN
                    base = sp.value_load(item_i[0:1, 1, bass.ds(w - 5, 1)], min_val=0, max_val=N)
                    sp.wait_ge(v_out, done(w, 5))
                    alone(sp, sp_passed)
                    if not (isinstance(w, int) and w == 5):
                        sp.wait_ge(stored, ((w - 5)) * 16)
                        alone(sp, sp_passed)
                    sp.dma_start(out[bass.ds(base, P), :], ob[:, s]).then_inc(stored, 16)
                if lo <= 0 < hi:
                    s = j
                    if not (isinstance(w, int) and w < UN):
                        sp.wait_ge(v_last, done(w, 3))
                        alone(sp, sp_passed)
                        sp.wait_ge(v_diff, done(w, 3))
                        alone(sp, sp_passed)
                        sp.wait_ge(v_dl, done(w, 3))
                        alone(sp, sp_passed)
                        sp.wait_ge(pe_z, done(w, 3, 4, 4))
                        alone(sp, sp_passed)
                    g = sp.value_load(item_i[0:1, 0, bass.ds(w, 1)], min_val=0, max_val=G - 1)
                    sp.dma_start(edg[:, s], edges[:, bass.ds(g, 1)].rearrange("p a k c -> p (a k) c")).then_inc(idx_loaded[s], 16)
                    sp.dma_start(drow[0:CH * H, s, :], dst_row[bass.ds(g, 1)].rearrange("a c e -> (a c) e")).then_inc(idx_loaded[s], 16)
                if lo <= 1 < hi:
                    s = (j - 1) % UN
                    if not (isinstance(w, int) and w < 4):
                        sp.wait_ge(pe_z, done(w, 4, 4, 4))
                        alone(sp, sp_passed)
                    g = sp.value_load(item_i[0:1, 0, bass.ds(w - 1, 1)], min_val=0, max_val=G - 1)
                    base = sp.value_load(item_i[0:1, 1, bass.ds(w - 1, 1)], min_val=0, max_val=N)
                    sp.dma_start(ea[:, s], ea_t[:, bass.ds(g, 1), :].rearrange("p a e -> p (a e)")).then_inc(ea_loaded[s], 16)
                    sp.dma_start(xrw[:, s], xr_tab[bass.ds(base, P)]).then_inc(ea_loaded[s], 16)
                if lo <= 3 < hi:
                    s = (j - 3) % UN
                    if not (isinstance(w, int) and w < 6):
                        sp.wait_ge(v_y1, done(w, 6))
                        alone(sp, sp_passed)
                    base = sp.value_load(item_i[0:1, 1, bass.ds(w - 3, 1)], min_val=0, max_val=N)
                    sp.dma_start(xw[:, s], x[bass.ds(base, P), :]).then_inc(xw_loaded[s], 16)

            n_items = items(sp, step, 6)
            sp.wait_ge(stored, n_items * 16)
            alone(sp, sp_passed)

        @block.gpsimd
        def _(pool):
            nc.gpsimd.memset(ones[:], 1.0).then_inc(consts, 1)
            nc.gpsimd.iota(iota_w[:], pattern=[[1, WT]], base=0, channel_multiplier=0,
                           allow_small_or_imprecise_dtypes=True).then_inc(consts, 1)
            nc.gpsimd.iota(iota_p[:], pattern=[[0, 1]], base=0, channel_multiplier=1,
                           allow_small_or_imprecise_dtypes=True).then_inc(consts, 1)
            nc.gpsimd.iota(node_no[:], pattern=[[1, P], [0, CW]], base=0, channel_multiplier=0,
                           allow_small_or_imprecise_dtypes=True).then_inc(consts, 1)
            pool.wait_ge(consts, 4)
            nc.gpsimd.affine_select(out=tri[:], in_=ones[:], compare_op=ALU.is_ge, fill=0.0, base=0,
                                    pattern=[[1, P]], channel_multiplier=-1).then_inc(consts, 1)
            nc.gpsimd.affine_select(out=ident[:], in_=ones[:], compare_op=ALU.is_equal, fill=0.0, base=0,
                                    pattern=[[1, P]], channel_multiplier=-1).then_inc(consts, 1)

            def normalise(b, s):
                pool.wait_ge(p_rstd, b + 1)
                if not (isinstance(b, int) and b < 2):
                    pool.wait_ge(p_tr, b - 1)
                alone(pool, pool_passed)
                for k in range(NB):
                    ins = nc.gpsimd.tensor_scalar(phn[:, s, k], px[:, s, k], pmv[:, s, k, 0:1], prs[:, s, k:k + 1],
                                                  ALU.subtract, ALU.mult)
                ins.then_inc(p_hn, 1)

            def split(b, s):
                pool.wait_ge(p_hi, b + 1)
                nc.gpsimd.tensor_tensor(pres[:, s], pf[:, s, :, D:2 * D], pxr[:, s, :, 0], ALU.subtract).then_inc(p_res, 1)
                pool.wait_ge(p_mid, b + 1)
                nc.gpsimd.tensor_tensor(pxr[:, s, :, 2], pres[:, s], pxr[:, s, :, 1], ALU.subtract).then_inc(p_low, 1)

            normalise(0, 0)
            for b in range(1, 4):
                normalise(b, b % 2)
                split(b - 1, (b - 1) % 2)
            with pool.Fori(4, BATCHES, 2) as b0:
                for s in range(2):
                    normalise(b0 + s, s)
                    split(b0 + (s - 1), 1 - s)
            split(BATCHES - 1, 1)
            for s in range(2):
                pool.wait_ge(p_stored[s], 16 * BATCHES)

            def gathers(w, j, r):
                pool.wait_ge(idx_loaded[j], in_slot(r, j, 0, 32))
                if not (isinstance(w, int) and w < UN):
                    pool.wait_ge(v_msg, done(w, 3))
                alone(pool, pool_passed)
                for c in range(CH):
                    pool.indirect_dma_start(
                        out=gx[:, j, c, :], out_offset=None, in_=xl_tab,
                        in_offset=bass.IndirectOffsetOnAxis(ap=edg[:, j, 0, c:c + 1], axis=0),
                    ).then_inc(gathered[j], 16)

            items(pool, lambda w, j, r, lo, hi: gathers(w, j, r), 1)

        @block.tensor
        def _(pe):
            pe.wait_ge(consts, 6)
            pe.wait_ge(ptab, 1)
            pe.matmul(pch[:, 0:1], tri[:], bnd_f[:, 0:1], start=True, stop=True).then_inc(tab_ps, 1)
            pe.wait_ge(ptab, 2)
            pe.matmul(pch[:, 0:WT], ones[:], tabs[:, 0, :], start=True, stop=True).then_inc(tab_ps, 1)
            pe.matmul(pag[:, 0:WT], ones[:], tabs[:, 1, :], start=True, stop=True).then_inc(tab_ps, 1)
            pe.matmul(pnd[:, 0:WT], ones[:], tabs[:, 2, :], start=True, stop=True).then_inc(tab_ps, 1)
            pe.wait_ge(ptab, 3)
            pe.matmul(pch[:, 0:1], ones[:], bnd_f[:, 0:1], start=True, stop=True).then_inc(tab_ps, 1)

            pe.wait_ge(scaled, 3)
            pe.wait_ge(tables, 1)

            def p_batch(b, s):
                tr = (pch, pag)[s]
                pe.wait_ge(p_hn, b + 1)
                if not (isinstance(b, int) and b < 2):
                    pe.wait_ge(p_ht, b - 1)
                for k in range(NB):
                    ins = pe.transpose(tr[:, k * P:(k + 1) * P], phn[:, s, k], ident[:])
                ins.then_inc(p_tr, 1)
                pe.wait_ge(p_ht, b + 1)
                if not (isinstance(b, int) and b < 1):
                    pe.wait_ge(p_add, 2 * b)
                for k in range(NB):
                    bank = pz[:, k // 2].rearrange("p a d -> p (a d)")
                    ins = pe.matmul(bank[:, (k % 2) * 2 * D:(k % 2 + 1) * 2 * D], pht[:, s, k * P:(k + 1) * P],
                                    w_lr[:], start=k % 2 == 0, stop=k % 2 == 1)
                    if k % 2:
                        ins.then_inc(p_mm, 1)

            p_batch(0, 0)
            p_batch(1, 1)
            with pe.Fori(2, BATCHES, 2) as b0:
                for s in range(2):
                    p_batch(b0 + s, s)

            def z_start(w, j, q):
                c0, n = GROUPS[q]
                bank = pz[:, (4 * j + q) % 3]
                if isinstance(w, int) and 4 * w + q < 3:
                    pe.wait_ge(p_add, 2 * BATCHES)
                else:
                    pe.wait_ge(v_leak, w * 4 + (q - 2))
                for k in range(n):
                    pe.matmul(bank[:, k], ea[:, j, (c0 + k) * P:(c0 + k + 1) * P], w_e[:], start=k == 0, stop=False)
                    pe.matmul(bank[:, k], ident[:], gx[:, j, c0 + k], start=False, stop=False)

            def z_end(w, j, q):
                c0, n = GROUPS[q]
                bank = pz[:, (4 * j + q) % 3]
                for k in range(n):
                    for part in range(3):
                        ins = pe.matmul(bank[:, k], mt[:, j, (c0 + k) * P:(c0 + k + 1) * P], xrw[:, j, part],
                                        start=False, stop=k == n - 1 and part == 2)
                ins.then_inc(pe_z, 1)

            def step(w, j, r, lo, hi):
                a, b, c = lo <= 0 < hi, lo <= 1 < hi, lo <= 2 < hi
                v, u = (j - 1) % UN, (j - 2) % UN
                if b:
                    pe.wait_ge(v_lg, done(w, 1, 2, 2))
                    pe.transpose(ch_lt[0:CH * H], lg[:, v, :], ident[:]).then_inc(pe_lt, 1)
                if a:
                    pe.wait_ge(ea_loaded[j], in_slot(r, j, 0, 32))
                    pe.wait_ge(gathered[j], in_slot(r, j, 0, 16 * CH))
                    z_start(w, j, 0)
                    pe.wait_ge(v_m, done(w, 0))
                    if not (isinstance(w, int) and w < 1):
                        pe.wait_ge(a_mt, done(w, 1, 2, 2))
                    for k in range(CH):
                        ins = pe.transpose(pmt[:, k // 8, (k % 8) * P:(k % 8 + 1) * P], m16[:, j, :, k], ident16[:])
                        if k in (7, CH - 1):
                            ins.then_inc(pe_mt, 1)
                if b:
                    if c:
                        pe.wait_ge(v_acc, done(w, 2))
                        pe.wait_ge(v_sel, done(w, 2))
                    pe.matmul(carry, sel[:, u], accs[:, u], start=True, stop=True).then_inc(pe_carry, 1)
                    pe.wait_ge(v_scan, done(w, 1))
                    pe.transpose(ch_vt, scan[0:CH * H, :], ident[0:CH * H, 0:CH * H]).then_inc(pe_vt, 1)
                if a:
                    z_start(w, j, 1)
                    pe.wait_ge(a_mt, done(w, 0, 2, 2))
                    z_end(w, j, 0)
                if b:
                    pe.wait_ge(v_low, done(w, 1))
                    pe.wait_ge(a_hi, done(w, 1))
                    for k in range(CH):
                        o = ch_cand[:, 9 * k:9 * k + 9]
                        pe.matmul(o, m16[:, v, :, k], vs[:, v, k, 0:9], start=True, stop=False, skip_group_check=True)
                        ins = pe.matmul(o[:, 0:H], m16[:, v, :, k], vs[:, v, k, 9:17], start=False, stop=True,
                                        skip_group_check=True)
                    ins.then_inc(pe_sel, 1)
                if a:
                    z_end(w, j, 1)
                    z_start(w, j, 2)
                    z_end(w, j, 2)
                if b:
                    pe.wait_ge(v_mlo, done(w, 1))
                    for k in range(CH):
                        o = ch_sh[:, H * k:H * k + H]
                        for part in range(2):
                            ins = pe.matmul(o, mt[:, v, k * P:(k + 1) * P], ms[:, part * H:(part + 1) * H],
                                            start=part == 0, stop=part == 1, skip_group_check=True)
                    ins.then_inc(pe_sh, 1)
                if c:
                    pe.wait_ge(v_hn, done(w, 2))
                    pe.transpose(pnd[:, 0:P], hn[:], ident[:]).then_inc(pe_ht, 1)
                if a:
                    z_start(w, j, 3)
                    z_end(w, j, 3)
                if c:
                    pe.wait_ge(a_hnt, done(w, 2))
                    for k in range(4):
                        ins = pe.matmul(pnd[:, k * P:(k + 1) * P], w_fc[:, k * P:(k + 1) * P], hnt[:],
                                        start=k == 0, stop=k == 3)
                    ins.then_inc(pe_fc, 1)
                if b:
                    pe.wait_ge(v_msg, done(w, 1))
                    pe.wait_ge(a_m32, done(w, 1))
                    for k in range(CH):
                        ins = pe.matmul(aggr, m32[:, v, k], msg[:, k * H:(k + 1) * H].rearrange("p a b -> p (a b)"),
                                        start=k == 0, stop=k == CH - 1)
                    ins.then_inc(pe_agg, 1)
                if c:
                    pe.wait_ge(a_hid, done(w, 2))
                    for k in range(4):
                        ins = pe.matmul(pnd[:, 0:D], hid[:, k], w_pr[:, k], start=k == 0, stop=k == 3)
                    ins.then_inc(pe_proj, 1)

            items(pe, step, 3)

        @block.scalar
        def _(act):
            act.wait_ge(tables, 1)
            def evacuate(b, s):
                act.wait_ge(p_stats, NB * b + NB)
                if not (isinstance(b, int) and b < 2):
                    act.wait_ge(p_hn, b - 1)
                nc.scalar.activation(plv[:, s], pmv[:, s, :, 1], ACT.Ln, bias=eps_t[:]).then_inc(p_ln, 1)
                act.wait_ge(p_ln, b + 1)
                nc.scalar.activation(prs[:, s], plv[:, s], ACT.Exp, scale=-0.5).then_inc(p_rstd, 1)
                act.wait_ge(p_tr, b + 1)
                if not (isinstance(b, int) and b < 2):
                    act.wait_ge(p_mm, 2 * b - 2)
                nc.scalar.activation(pht[:, s], (pch, pag)[s][:], ACT.Copy).then_inc(p_ht, 1)

            def parts(b, s):
                act.wait_ge(p_add, 2 * b + 2)
                if not (isinstance(b, int) and b < 2):
                    act.wait_ge(p_stored[s], (b - s) * 16)
                nc.scalar.activation(pxr[:, s, :, 0], pf[:, s, :, D:2 * D], ACT.Copy).then_inc(p_hi, 1)
                act.wait_ge(p_res, b + 1)
                nc.scalar.activation(pxr[:, s, :, 1], pres[:, s], ACT.Copy).then_inc(p_mid, 1)

            evacuate(0, 0)
            for b in range(1, 4):
                evacuate(b, b % 2)
                parts(b - 1, (b - 1) % 2)
            with act.Fori(4, BATCHES, 2) as b0:
                for s in range(2):
                    evacuate(b0 + s, s)
                    parts(b0 + (s - 1), 1 - s)
            parts(BATCHES - 1, 1)

            def relu(w, j, q):
                c0, n = GROUPS[q]
                if not (isinstance(w, int) and w < 1):
                    act.wait_ge(v_leak, w * 4 + (q - 3))
                act.wait_ge(pe_z, w * 4 + (q + 1))
                nc.scalar.activation(zr[:, c0:c0 + n], pz[:, (4 * j + q) % 3, 0:n], ACT.Relu).then_inc(a_relu, 1)

            def rstd(k, ready, got_ln, got):
                act.wait_ge(*ready)
                nc.scalar.activation(ln_v[:, k:k + 1], mv2[:, k, 1:2], ACT.Ln, bias=eps_t[:]).then_inc(a_ln, 1)
                act.wait_ge(a_ln, got_ln)
                nc.scalar.activation(rs2[:, k:k + 1], ln_v[:, k:k + 1], ACT.Exp, scale=-0.5).then_inc(a_rs, 1)

            def step(w, j, r, lo, hi):
                a, b, c, d = (lo <= k < hi for k in range(4))
                v, u = (j - 1) % UN, (j - 2) % UN
                if a:
                    act.wait_ge(v_diff, done(w, 0))
                    nc.scalar.activation(runf[0:CH * H, j], runf[0:CH * H, j], ACT.Copy, scale=BIG).then_inc(a_runf, 1)
                    for k, n in ((0, 8), (1, CH - 8)):
                        act.wait_ge(pe_mt, w * 2 + (k + 1))
                        nc.scalar.activation(mt[:, j, k * 8 * P:(k * 8 + n) * P], pmt[:, k, 0:n * P],
                                             ACT.Copy).then_inc(a_mt, 1)
                if b:
                    act.wait_ge(v_vlast, done(w, 1))
                    nc.scalar.activation(vs[:, v, :, 0:H], vlast[:], ACT.Copy).then_inc(a_hi, 1)
                if a:
                    relu(w, j, 0)
                if d:
                    n = done(w, 3, 2, 2)
                    rstd(1, (v_mvf, done(w, 3)), n, n)
                if a:
                    relu(w, j, 1)
                if c:
                    n = done(w, 2, 1, 2)
                    rstd(0, (v_mv, done(w, 2)), n, n)
                if a:
                    act.wait_ge(v_m, done(w, 0))
                    nc.scalar.activation(m32[:, j], m16[:, j].rearrange("p n c -> p c n")[:, 0:CH], ACT.Copy).then_inc(a_m32, 1)
                    relu(w, j, 2)
                if c:
                    act.wait_ge(pe_ht, done(w, 2))
                    nc.scalar.activation(hnt[:], pnd[:, 0:P], ACT.Copy).then_inc(a_hnt, 1)
                if b:
                    act.wait_ge(v_farg, done(w, 1))
                    nc.scalar.activation(fac[:, v], farg[:], ACT.Exp).then_inc(a_fac, 1)
                if a:
                    relu(w, j, 3)
                if b:
                    act.wait_ge(v_dmin, done(w, 1))
                    if not (isinstance(w, int) and w < 2):
                        act.wait_ge(pe_agg, done(w, 2))
                    nc.scalar.activation(msg[:, :, HC], dmin[:], ACT.Exp).then_inc(a_exp, 1)
                if c:
                    act.wait_ge(pe_fc, done(w, 2))
                    nc.scalar.activation(hid[:].rearrange("p a n -> p (a n)"), pnd[:], ACT.Relu).then_inc(a_hid, 1)

            items(act, step, 4)

        @block.vector
        def _(dve):
            V = nc.vector
            dve.wait_ge(w_loaded, 16 * LOADS)
            dve.wait_ge(consts, 6)
            t = [0]

            def link(ins):
                t[0] += 1
                ins.then_inc(scaled_t, 1)
                dve.wait_ge(scaled_t, t[0])

            link(V.tensor_tensor(bnd_d[:], bnd[:, 1:2], bnd[:, 0:1], ALU.subtract))
            link(V.tensor_scalar(bnd_d[:], bnd_d[:], 7, None, ALU.arith_shift_right))
            V.tensor_scalar(bnd_f[:, 0:1], bnd_d[:], 1.0, None, ALU.add).then_inc(ptab, 1)
            dve.wait_ge(tab_ps, 1)
            link(V.tensor_copy(bnd_f[:, 1:2], pch[:, 0:1]))
            link(V.tensor_tensor(bnd_f[:, 2:3], bnd_f[:, 1:2], bnd_f[:, 0:1], ALU.subtract))
            link(V.tensor_copy(bnd_f[:, 3:4], bnd[:, 0:1]))
            link(V.scalar_tensor_tensor(bnd_f[:, 4:5], bnd_f[:, 2:3], -float(P), bnd_f[:, 3:4], ALU.mult, ALU.add))
            link(V.tensor_scalar(tabs[:, 3, :], iota_w[:], bnd_f[:, 2:3], None, ALU.is_ge))
            link(V.scalar_tensor_tensor(tabs[:, 1, :], iota_w[:], bnd_f[:, 1:2], tabs[:, 3, :], ALU.is_lt, ALU.mult))
            link(V.tensor_scalar(tabs[:, 3, :], iota_w[:], float(P), bnd_f[:, 4:5], ALU.mult, ALU.add))
            link(V.tensor_tensor(tabs[:, 0, :], tabs[:, 3, :], tabs[:, 1, :], ALU.mult))
            V.tensor_scalar(tabs[:, 2, :], iota_w[:], bnd_f[:, 1:2], None, ALU.is_ge).then_inc(ptab, 1)
            dve.wait_ge(tab_ps, 4)
            link(V.tensor_scalar(tabs[:, 3, :], pag[:, 0:WT], -float(N), float(N), ALU.mult, ALU.add))
            link(V.tensor_tensor(base_f[:], tabs[:, 3, :], pch[:, 0:WT], ALU.add))
            link(V.tensor_scalar(item_i[:, 0, :], pnd[:, 0:WT], float(G - 1), None, ALU.min))
            link(V.tensor_copy(item_i[:, 1, :], base_f[:]))
            link(V.memset(delta_f[:], 0.0))
            V.tensor_tensor(delta_f[:, 0:WT - 1], base_f[:, 1:WT], base_f[:, 0:WT - 1], ALU.subtract).then_inc(ptab, 1)
            dve.wait_ge(tab_ps, 5)
            link(V.tensor_copy(bnd_f[:, 5:6], pch[:, 0:1]))
            link(V.tensor_scalar(cnt_f[:, 0, :], iota_w[:, 0:P], float(UN), bnd_f[:, 5:6], ALU.mult, ALU.is_lt))
            link(V.tensor_reduce(bnd_f[:, 6:7], cnt_f[:, 0, :], AX.X, ALU.add))
            link(V.tensor_scalar(more_i[:], bnd_f[:, 6:7], float(-(G // UN)), None, ALU.add))
            V.tensor_scalar(w_lr[:], w_lr[:], ln1[:], None, ALU.mult).then_inc(scaled, 1)
            V.tensor_scalar(w_fc[:], w_fc[:], ln2[:], None, ALU.mult).then_inc(scaled, 1)
            V.tensor_copy(ident16[:], ident[:]).then_inc(scaled, 1)
            link(V.tensor_scalar(att_b[:], att_b[:], 1.0 - SLOPE, None, ALU.mult))
            link(V.memset(sel[:], 0.0))
            link(V.memset(accs[:], 0.0))
            link(V.memset(accs[:, :, AW + H:AW + H + 1], 1.0))
            link(V.memset(runf[:], 0.0))
            link(V.memset(vs[:], 0.0))
            V.memset(eps_t[:], EPS).then_inc(tables, 1)
            dve.wait_ge(tables, 1)

            def stats(b, s, n):
                dve.wait_ge(px_loaded[s], n)
                if not (isinstance(b, int) and b < 2):
                    dve.wait_ge(p_hn, b - 1)
                for k in range(NB):
                    ins = V.bn_stats(pst[:, s, k], px[:, s, k])
                ins.then_inc(p_bn, 1)
                dve.wait_ge(p_bn, b + 1)
                alone(dve, dve_passed)
                for k in range(NB):
                    V.bn_aggr(pmv[:, s, k], pst[:, s, k]).then_inc(p_stats, 1)

            def bias(b, s):
                if not (isinstance(b, int) and b < 2):
                    dve.wait_ge(p_stored[s], (b - s) * 16)
                for k in range(2):
                    dve.wait_ge(p_mm, 2 * b + (k + 1))
                    V.tensor_tensor(pf[:, s, 2 * k:2 * k + 2], pz[:, k].rearrange("p (t a) d -> p t (a d)", t=2),
                                    b_lr[:].unsqueeze(1).broadcast_to([P, 2, 2 * D]), ALU.add).then_inc(p_add, 1)

            stats(0, 0, 16)
            for b in range(1, 4):
                stats(b, b % 2, b // 2 * 16 + 16)
                bias(b - 1, (b - 1) % 2)
            with dve.Fori(4, BATCHES, 2) as b0:
                for s in range(2):
                    stats(b0 + s, s, b0 * 8 + 16)
                    bias(b0 + (s - 1), 1 - s)
            bias(BATCHES - 1, 1)

            def leaky(w, j, q):
                c0, n = GROUPS[q]
                dve.wait_ge(a_relu, w * 4 + (q + 1))
                V.scalar_tensor_tensor(zl[:, c0:c0 + n], pz[:, (4 * j + q) % 3, 0:n], SLOPE / (1.0 - SLOPE), zr[:, c0:c0 + n],
                                       ALU.mult, ALU.add).then_inc(v_leak, 1)

            def times_att(w, q):
                c0, n = GROUPS[q]
                dve.wait_ge(v_leak, w * 4 + (q + 1))
                V.tensor_tensor(zl[:, c0:c0 + n], zl[:, c0:c0 + n], att_b[:].unsqueeze(1).broadcast_to([P, n, D]),
                                ALU.mult).then_inc(v_att, 1)

            def logits(w, j, half):
                c0, n = ((0, 8), (8, CH - 8))[half]
                dve.wait_ge(v_att, w * 4 + (2 * half + 2))
                V.tensor_reduce(lg[:, j, c0 * H:(c0 + n) * H], zl[:, c0:c0 + n].rearrange("p c (h k) -> p (c h) k", k=HC),
                                AX.X, ALU.add).then_inc(v_lg, 1)

            def step(w, j, r, lo, hi):
                a, b, c, d = (lo <= k < hi for k in range(4))
                v, u, y = (j - 1) % UN, (j - 2) % UN, (j - 3) % UN
                if a:
                    dve.wait_ge(idx_loaded[j], in_slot(r, j, 0, 32))
                    V.tensor_scalar(dl[:, j], edg[:, j, 1], base_f[:, bass.ds(w, 1)], None, ALU.subtract).then_inc(v_dl, 1)
                    if not (isinstance(w, int) and w < UN):
                        dve.wait_ge(pe_sel, done(w, 3))
                    V.tensor_tensor(vs[:, j, :, H], edg[:, j, 1, 0:CH], edg[:, j, 2, 0:CH], ALU.not_equal).then_inc(v_last, 1)
                    V.tensor_tensor(runf[0:CH * H, j, 1:P], drow[0:CH * H, j, 0:P - 1], drow[0:CH * H, j, 1:P],
                                    ALU.subtract).then_inc(v_diff, 1)
                if c:
                    dve.wait_ge(pe_agg, done(w, 2))
                    dve.wait_ge(a_fac, done(w, 2))
                    V.tensor_tensor(tmpa[:].rearrange("p (h k) -> p h k", k=MS),
                                    carry[:, 0:AW].rearrange("p (h k) -> p h k", k=MS),
                                    fac[:, u].unsqueeze(2).broadcast_to([P, H, MS]), ALU.mult).then_inc(v_tmp, 1)
                if a:
                    dve.wait_ge(v_dl, done(w, 0))
                    V.tensor_tensor(m16[:, j], dl[:, j].unsqueeze(1).broadcast_to([P, P, CW]), node_no[:],
                                    ALU.is_equal).then_inc(v_m, 1)
                if b:
                    dve.wait_ge(pe_lt, done(w, 1))
                    dve.wait_ge(a_runf, done(w, 1))
                    V.tensor_tensor_scan(scan[0:CH * H, :], runf[0:CH * H, v], ch_lt[0:CH * H], -BIG,
                                         ALU.add, ALU.max).then_inc(v_scan, 1)
                if c:
                    dve.wait_ge(v_tmp, done(w, 2))
                    V.tensor_tensor(accs[:, u, 0:AW], tmpa[:], aggr, ALU.add).then_inc(v_acc, 1)
                    V.tensor_scalar(sel[:, u, 0:1], iota_p[:], delta_f[:, bass.ds(w - 2, 1)], None,
                                    ALU.is_equal).then_inc(v_sel, 1)
                    dve.wait_ge(xw_loaded[u], in_slot(r, j, 2, 16))
                    V.tensor_tensor(xab[:], xw[:, u], a_bias[:], ALU.add).then_inc(v_xab, 1)
                if d:
                    dve.wait_ge(v_y1, done(w, 3))
                    dve.wait_ge(pe_proj, done(w, 3))
                    V.tensor_tensor(y1[:, y], y1[:, y], pnd[:, 0:D], ALU.add).then_inc(v_y, 1)
                if c:
                    dve.wait_ge(v_acc, done(w, 2))
                    V.tensor_scalar(rden[:, 0], accs[:, u, HC:AW:MS], 1e-30, None, ALU.max).then_inc(v_den, 1)
                if b:
                    dve.wait_ge(pe_vt, done(w, 1))
                    V.tensor_tensor(vlast[:], ch_vt.rearrange("p (c h) -> p c h", h=H),
                                    vs[:, v, :, H:H + 1].broadcast_to([P, CH, H]), ALU.mult).then_inc(v_vlast, 1)
                if c:
                    dve.wait_ge(v_den, done(w, 2))
                    V.reciprocal(rden[:, 1], rden[:, 0]).then_inc(v_rden, 1)
                if d:
                    dve.wait_ge(v_y, done(w, 3))
                    V.bn_stats(st2[:, 1], y1[:, y]).then_inc(v_stf, 1)
                if c:
                    dve.wait_ge(v_rden, done(w, 2))
                    V.tensor_tensor(attn[:].rearrange("p (h k) -> p h k", k=HC),
                                    accs[:, u, 0:AW].rearrange("p (h k) -> p h k", k=MS)[:, :, 0:HC],
                                    rden[:, 1].unsqueeze(2).broadcast_to([P, H, HC]), ALU.mult).then_inc(v_attn, 1)
                if b:
                    dve.wait_ge(a_hi, done(w, 1))
                    V.tensor_tensor(vs[:, v, :, H + 1:2 * H + 1], vlast[:], vs[:, v, :, 0:H], ALU.subtract).then_inc(v_low, 1)
                if d:
                    dve.wait_ge(v_stf, done(w, 3))
                    alone(dve, dve_passed)
                    V.bn_aggr(mv2[:, 1], st2[:, 1]).then_inc(v_mvf, 1)
                if c:
                    dve.wait_ge(v_attn, done(w, 2))
                    V.tensor_tensor(x1[:, u], attn[:], xab[:], ALU.add).then_inc(v_x1, 1)
                if a:
                    leaky(w, j, 0)
                if c:
                    dve.wait_ge(v_x1, done(w, 2))
                    V.bn_stats(st2[:, 0], x1[:, u]).then_inc(v_st, 1)
                if b:
                    dve.wait_ge(pe_sel, done(w, 1))
                    V.tensor_scalar(pen[:], ch_cand.rearrange("p (c k) -> p c k", k=9)[:, :, 8], -1.0, BIG,
                                    ALU.add, ALU.mult).then_inc(v_pen, 1)
                    dve.wait_ge(pe_carry, done(w, 1))
                    V.tensor_scalar(pen2[:], carry[:, AW + H:AW + H + 1], -1.0, BIG, ALU.add, ALU.mult).then_inc(v_pen2, 1)
                if c:
                    dve.wait_ge(v_st, done(w, 2))
                    alone(dve, dve_passed)
                    V.bn_aggr(mv2[:, 0], st2[:, 0]).then_inc(v_mv, 1)
                if b:
                    dve.wait_ge(v_pen, done(w, 1))
                    V.tensor_tensor(cand[:], ch_cand.rearrange("p (c k) -> p c k", k=9)[:, :, 0:8],
                                    pen[:].unsqueeze(2).broadcast_to([P, CH, H]), ALU.add).then_inc(v_cand, 1)
                if a:
                    times_att(w, 0)
                if b:
                    dve.wait_ge(v_cand, done(w, 1))
                    V.tensor_reduce(mblk[:], cand[:].rearrange("p c h -> p h c"), AX.X, ALU.max).then_inc(v_mblk, 1)
                if a:
                    leaky(w, j, 1)
                if b:
                    dve.wait_ge(v_mblk, done(w, 1))
                    V.scalar_tensor_tensor(accs[:, v, AW:AW + H], carry[:, AW:AW + H], pen2[:], mblk[:],
                                           ALU.add, ALU.max).then_inc(v_max, 1)
                if a:
                    times_att(w, 1)
                if b:
                    dve.wait_ge(v_max, done(w, 1))
                    V.tensor_copy(ms[:, 0:H], accs[:, v, AW:AW + H]).then_inc(v_mhi, 1)
                    V.scalar_tensor_tensor(farg[:], carry[:, AW:AW + H], pen2[:], accs[:, v, AW:AW + H],
                                           ALU.add, ALU.subtract).then_inc(v_farg, 1)
                    dve.wait_ge(v_mhi, done(w, 1))
                    V.tensor_tensor(ms[:, H:2 * H], accs[:, v, AW:AW + H], ms[:, 0:H], ALU.subtract).then_inc(v_mlo, 1)
                if c:
                    dve.wait_ge(a_rs, done(w, 2, 1, 2))
                    V.tensor_scalar(hn[:], x1[:, u], mv2[:, 0, 0:1], rs2[:, 0:1], ALU.subtract, ALU.mult).then_inc(v_hn, 1)
                    V.tensor_tensor(y1[:, u], x1[:, u], xw[:, u], ALU.add).then_inc(v_y1, 1)
                if d:
                    dve.wait_ge(a_rs, done(w, 3, 2, 2))
                    if not (isinstance(w, int) and w < 6):
                        dve.wait_ge(stored, (w - 5) * 16)
                    V.tensor_scalar(ob[:, y], y1[:, y], mv2[:, 1, 0:1], rs2[:, 1:2], ALU.subtract, ALU.mult).then_inc(v_out, 1)
                if a:
                    leaky(w, j, 2)
                if b:
                    dve.wait_ge(pe_sh, done(w, 1))
                    V.tensor_tensor(dlt[:], lg[:, v], ch_sh, ALU.subtract).then_inc(v_dlt, 1)
                if a:
                    times_att(w, 2)
                if b:
                    dve.wait_ge(v_dlt, done(w, 1))
                    V.tensor_scalar(dmin[:], dlt[:], 0.0, None, ALU.min).then_inc(v_dmin, 1)
                if a:
                    logits(w, j, 0)
                    leaky(w, j, 3)
                if b:
                    dve.wait_ge(a_exp, done(w, 1))
                    V.tensor_tensor(msg[:, :, 0:HC], gx[:, v].rearrange("p c (h k) -> p (c h) k", k=HC),
                                    msg[:, :, HC:MS].broadcast_to([P, CH * H, HC]), ALU.mult).then_inc(v_msg, 1)
                if a:
                    times_att(w, 3)
                    logits(w, j, 1)

            items(dve, step, 4)


def kernel(x, src, dst, edge_attr_128, L0_gnn_ln1_w, L0_gnn_lin_l_w, L0_gnn_lin_l_b, L0_gnn_lin_r_w,
           L0_gnn_lin_r_b, L0_gnn_lin_edge_w, L0_gnn_att, L0_gnn_attn_bias, L0_gnn_ln2_w, L0_gnn_fc_w,
           L0_gnn_proj_w):
    import numpy as np
    import concourse.bacc as bacc
    from concourse.bass_utils import run_bass_kernel_spmd

    a = lambda v: np.asarray(v)
    xs = np.zeros((NP, D), np.float32)
    xs[:N] = a(x)
    ea_t = np.zeros((D, EP), np.float32)
    ea_t[:, :E] = a(edge_attr_128).T
    src_p, dst_p = np.zeros(EP, np.int32), np.full(EP, -1, np.int32)
    src_p[:E], dst_p[:E] = a(src), a(dst)
    edges = np.full((P, G, 3, CW), -1, np.int32)
    edges[:, :, 0, :CH] = src_p.reshape(G, CH, P).transpose(2, 0, 1)
    edges[:, :, 0, CH:] = 0
    edges[:, :, 1, :CH] = dst_p.reshape(G, CH, P).transpose(2, 0, 1)
    edges[:-1, :, 2, :CH] = edges[1:, :, 1, :CH]
    edges[-1, :, 2, :] = -2
    dst_row = np.repeat(dst_p.reshape(G, CH, P), H, axis=1)
    bounds = np.zeros((P, 2), np.int32)
    bounds[:, 1] = -P
    ends = dst_p[EG - 1:E:EG][:G - 1]
    bounds[1:G, 0] = ends
    bounds[:G - 1, 1] = ends
    bounds[G - 1, 1] = N - 1
    arrays = {
        "x": xs,
        "ea_t": ea_t.reshape(D, G, EG),
        "edges": edges,
        "dst_row": dst_row,
        "bounds": bounds,
        "ln1_w": a(L0_gnn_ln1_w).reshape(D, 1),
        "wlr_t": np.concatenate([a(L0_gnn_lin_l_w).T, a(L0_gnn_lin_r_w).T], 1),
        "blr": np.concatenate([a(L0_gnn_lin_l_b), a(L0_gnn_lin_r_b)]).reshape(1, 2 * D),
        "we_t": a(L0_gnn_lin_edge_w).T,
        "att": a(L0_gnn_att).reshape(1, D),
        "attn_bias": a(L0_gnn_attn_bias).reshape(1, D),
        "ln2_w": a(L0_gnn_ln2_w).reshape(D, 1),
        "fc_t": a(L0_gnn_fc_w).T,
        "proj_t": a(L0_gnn_proj_w).T.reshape(4, P, D).transpose(1, 0, 2),
    }
    arrays = {k: np.ascontiguousarray(v) for k, v in arrays.items()}
    nc = bacc.Bacc("TRN2", target_bir_lowering=False, num_devices=1)
    args = {k: nc.dram_tensor(f"{k}_in", v.shape, mybir.dt.from_np(v.dtype), kind="ExternalInput").ap()
            for k, v in arrays.items()}
    out = nc.dram_tensor("out_rows", (NP, D), F32, kind="ExternalOutput").ap()
    gnn_kernel(nc, out=out, **args)
    r = run_bass_kernel_spmd(nc, [{f"{k}_in": v for k, v in arrays.items()}], core_ids=[0])
    return r.results[0]["out_rows"][:N]
```

```python
from contextlib import ExitStack

import concourse.bass as bass
from concourse import mybir

P = 128
N, E, D, H = 12500, 200000, 128, 8
HC = D // H
CH = 14
EG = CH * P
G = -(-E // EG)
EP = G * EG
CW = CH + CH % 2
GROUPS = [(0, 4), (4, 4), (8, 3), (11, 3)]
HALVES = [(0, 8), (8, CH - 8)]
UN = 4
NB = 3
UP = 3
BATCHES = 33
NP = BATCHES * NB * P
WT = 216
HID = 4 * D
MAX_ROUNDS = -(-(G + N // P) // UN)
MS = HC + 1
AW = H * MS
BIG = 1.0e30
EPS = 1e-05
SLOPE = 0.2
assert G <= P and G % UN == 0 and G // UN > 2 and NP >= N + P and MAX_ROUNDS * UN < WT

ALU = mybir.AluOpType
ACT = mybir.ActivationFunctionType
AX = mybir.AxisListType
F32 = mybir.dt.float32
BF16 = mybir.dt.bfloat16
I32 = mybir.dt.int32


def gnn_kernel(nc, x, ea_t, edges, dst_row, bounds, ln1_w, wlr_t, blr, we_t, att, attn_bias,
               ln2_w, fc_t, proj_t, out):
    xl_tab = nc.dram_tensor("xl_tab", (NP, D), F32, kind="Internal").ap()
    xr_tab = nc.dram_tensor("xr_tab", (NP, 3, D), BF16, kind="Internal").ap()

    with ExitStack() as ctx:
        def sb(name, shape, dt=F32):
            return ctx.enter_context(nc.sbuf_tensor(name, shape, dt))

        def ps(name, shape, dt=F32):
            return ctx.enter_context(nc.psum_tensor(name, shape, dt))

        def sem(name):
            return ctx.enter_context(nc.semaphore(name))

        def sems(name, n):
            return [sem(f"{name}{k}") for k in range(n)]

        ident = sb("ident", [P, P])
        ident16 = sb("ident16", [P, P], BF16)
        ones = sb("ones", [P, P])
        tri = sb("tri", [P, P])
        iota_p = sb("iota_p", [P, 1])
        iota_w = sb("iota_w", [P, WT])
        node_no = sb("node_no", [P, P, CW], BF16)
        w_lr = sb("w_lr", [P, 2 * D])
        b_lr = sb("b_lr", [P, 2 * D])
        w_e = sb("w_e", [P, D])
        w_fc = sb("w_fc", [P, HID])
        w_pr = sb("w_pr", [P, 4, D])
        att_b = sb("att_b", [P, D])
        a_bias = sb("a_bias", [P, D])
        ln1 = sb("ln1", [P, 1])
        ln2 = sb("ln2", [P, 1])
        bnd = sb("bnd", [P, 2], I32)
        bnd_d = sb("bnd_d", [P, 1], I32)
        bnd_f = sb("bnd_f", [P, 8])
        tabs = sb("tabs", [P, 4, WT])
        base_f = sb("base_f", [P, WT])
        delta_f = sb("delta_f", [P, WT])
        item_i = sb("item_i", [P, 2, WT], I32)
        cnt_f = sb("cnt_f", [P, 2, P])
        more_i = sb("more_i", [P, 1], I32)
        px = sb("px", [P, UP, NB, D])
        pst = sb("pst", [P, UP, NB, 6])
        pmv = sb("pmv", [P, UP, NB, 2])
        plv = sb("plv", [P, UP, NB])
        prs = sb("prs", [P, UP, NB])
        eps_t = sb("eps_t", [P, 1])
        phn = sb("phn", [P, UP, NB, D])
        pht = sb("pht", [P, UP, NB * P])
        pf = sb("pf", [P, UP, NB, 2 * D])
        pres = sb("pres", [P, UP, NB, D])
        pxr = sb("pxr", [P, UP, NB, 3, D], BF16)
        edg = sb("edg", [P, UN, 3, CW], I32)
        drow = sb("drow", [P, UN, P], I32)
        ea = sb("ea", [P, 2, EG])
        gx = sb("gx", [P, UN, CH, D])
        xrw = sb("xrw", [P, 2, 3, D], BF16)
        xw = sb("xw", [P, UN, D])
        dl = sb("dl", [P, 2, CW], BF16)
        runf = sb("runf", [P, 2, P])
        m16 = sb("m16", [P, 2, P, CW], BF16)
        m32 = sb("m32", [P, 2, CH, P])
        mt = sb("mt", [P, 2, CH * P], BF16)
        zr = sb("zr", [P, CH, D])
        zl = sb("zl", [P, CH, D])
        lg = sb("lg", [P, 2, CH * H])
        scan = sb("scan", [P, P])
        vlast = sb("vlast", [P, CH, H])
        vs = sb("vs", [P, 2, CH, 2 * H + 1], BF16)
        pen = sb("pen", [P, CH])
        cand = sb("cand", [P, CH, H])
        mblk = sb("mblk", [P, H])
        pen2 = sb("pen2", [P, 1])
        ms = sb("ms", [P, 2 * H], BF16)
        farg = sb("farg", [P, H])
        fac = sb("fac", [P, 2, H])
        dlt = sb("dlt", [P, CH * H])
        dmin = sb("dmin", [P, CH * H])
        msg = sb("msg", [P, CH * H, MS])
        accs = sb("accs", [P, 2, AW + H + 1])
        tmpa = sb("tmpa", [P, AW])
        sel = sb("sel", [P, 2, P])
        rden = sb("rden", [P, 2, H])
        attn = sb("attn", [P, D])
        xab = sb("xab", [P, D])
        x1 = sb("x1", [P, 2, D])
        y1 = sb("y1", [P, 2, D])
        st2 = sb("st2", [P, 2, 6])
        mv2 = sb("mv2", [P, 2, 2])
        ln_v = sb("ln_v", [P, 2])
        rs2 = sb("rs2", [P, 2])
        hn = sb("hn", [P, D])
        hnt = sb("hnt", [P, P])
        hid = sb("hid", [P, 4, P])
        ob = sb("ob", [P, 2, D])

        pz = ps("pz", [P, 2, 4, D])
        pmt = ps("pmt", [P, 2, 8 * P], BF16)
        pch = ps("pch", [P, 512])
        pag = ps("pag", [P, 512])
        pcy = ps("pcy", [P, 512])
        pnd = ps("pnd", [P, 512])
        ch_lt, ch_vt, ch_cand, ch_sh = pch[:, 0:P], pch[:, P:P + CH * H], pch[:, 248:248 + 9 * CH], pch[:, 384:384 + CH * H]
        carry, aggr = pcy[:, 0:AW + H + 1], pag[:, 0:AW]

        p_bank = (pch, pag, pcy)
        pz_rows = pz[:].rearrange("p b (t a) d -> p (b t) (a d)", a=2)

        w_loaded = sem("w_loaded")
        consts = sem("consts")
        scaled = sem("scaled")
        scaled_t = sem("table_steps")
        tables = sem("tables")
        tab_ps = sem("tab_ps")
        ptab = sem("ptab")
        px_loaded = sems("px_loaded", UP)
        p_stats = sem("p_stats")
        p_bn = sem("p_bn")
        p_rstd = sem("p_rstd")
        p_ln = sem("p_ln")
        p_hn = sem("p_hn")
        p_tr = sem("p_tr")
        p_ht = sem("p_ht")
        p_mm = sem("p_mm")
        p_add = sem("p_add")
        p_hi = sem("p_hi")
        p_res = sem("p_res")
        p_mid = sem("p_mid")
        p_low = sem("p_low")
        p_stored = sems("p_stored", UP)
        idx_loaded = sems("idx_loaded", UN)
        ea_loaded = sems("ea_loaded", 2)
        xw_loaded = sems("xw_loaded", UN)
        gathered = sems("gathered", UN)
        stored = sem("stored")
        pe_lt = sem("pe_lt"); pe_z = sem("pe_z"); pe_mt = sem("pe_mt"); pe_carry = sem("pe_carry")
        pe_vt = sem("pe_vt"); pe_sel = sem("pe_sel"); pe_sh = sem("pe_sh"); pe_ht = sem("pe_ht")
        pe_fc = sem("pe_fc"); pe_agg = sem("pe_agg"); pe_proj = sem("pe_proj")
        a_runf = sem("a_runf"); a_mt = sem("a_mt"); a_hi = sem("a_hi"); a_relu = sem("a_relu")
        a_ln = sem("a_ln"); a_rs = sem("a_rs"); a_m32 = sem("a_m32"); a_hnt = sem("a_hnt")
        a_hid = sem("a_hid"); a_fac = sem("a_fac"); a_exp = sem("a_exp")
        v_dl = sem("v_dl"); v_last = sem("v_last"); v_diff = sem("v_diff"); v_m = sem("v_m")
        v_scan = sem("v_scan"); v_tmp = sem("v_tmp"); v_acc = sem("v_acc"); v_vlast = sem("v_vlast")
        v_low = sem("v_low"); v_leak = sem("v_leak"); v_att = sem("v_att"); v_lg = sem("v_lg")
        v_pen = sem("v_pen"); v_cand = sem("v_cand"); v_mblk = sem("v_mblk"); v_max = sem("v_max")
        v_farg = sem("v_farg"); v_mhi = sem("v_mhi"); v_mlo = sem("v_mlo"); v_dlt = sem("v_dlt")
        v_dmin = sem("v_dmin"); v_msg = sem("v_msg"); v_den = sem("v_den"); v_rden = sem("v_rden")
        v_attn = sem("v_attn"); v_xab = sem("v_xab"); v_x1 = sem("v_x1"); v_st = sem("v_st")
        v_mv = sem("v_mv"); v_hn = sem("v_hn"); v_y1 = sem("v_y1")
        v_y = sem("v_y"); v_stf = sem("v_stf"); v_mvf = sem("v_mvf")
        v_out = sem("v_out"); v_pen2 = sem("v_pen2"); v_sel = sem("v_sel")

        LOADS = 10
        PEEL = 2 * UN

        def items(eng, body, depth):
            eng.wait_ge(tables, 1)
            more = eng.value_load(more_i[0:1, 0:1], min_val=0, max_val=MAX_ROUNDS - G // UN)
            n_rounds = eng.snap(more + G // UN)
            n_items = eng.snap(n_rounds * UN)
            for w in range(PEEL):
                body(w, w % UN, w // UN, 0, min(depth, w + 1))
            with eng.Fori(PEEL // UN, n_rounds) as r:
                w0 = eng.snap(r * UN)
                for j in range(UN):
                    body(w0 + j, j, r, 0, depth)
            for j in range(depth - 1):
                body(n_items + j, j % UN, n_rounds + j // UN, j + 1, depth)
            return n_items

        def done(w, back, n=1, per=1):
            return w * per + (n - back * per)

        def in_slot(r, j, back, slots, per):
            return r * (per * UN // slots) + ((j - back) // slots + 1) * per

        def batches(eng, body, depth):
            for b in range(2 * UP):
                body(b, b // UP, b % UP, 0, min(depth, b + 1))
            with eng.Fori(2, BATCHES // UP) as t:
                b0 = eng.snap(t * UP)
                for s in range(UP):
                    body(b0 + s, t, s, 0, depth)
            for s in range(depth - 1):
                body(BATCHES + s, BATCHES // UP, s, s + 1, depth)

        def group(w, q):
            return w * 4 + (q - 3)

        sp_passed, pool_passed, dve_passed = sem("sp_passed"), sem("pool_passed"), sem("dve_passed")

        def alone(eng, passed):
            eng.sem_inc(passed, 1)

        block = ctx.enter_context(nc.Block())

        @block.sync
        def _(sp):
            sp.dma_start(bnd[:], bounds).then_inc(w_loaded, 16)
            sp.dma_start(w_lr[:], wlr_t).then_inc(w_loaded, 16)
            sp.dma_start(b_lr[:], blr.broadcast_to([P, 2 * D])).then_inc(w_loaded, 16)
            sp.dma_start(ln1[:], ln1_w).then_inc(w_loaded, 16)
            sp.dma_start(ln2[:], ln2_w).then_inc(w_loaded, 16)
            sp.dma_start(w_e[:], we_t).then_inc(w_loaded, 16)
            sp.dma_start(w_fc[:], fc_t).then_inc(w_loaded, 16)
            sp.dma_start(w_pr[:], proj_t).then_inc(w_loaded, 16)
            sp.dma_start(att_b[:], att.broadcast_to([P, D])).then_inc(w_loaded, 16)
            sp.dma_start(a_bias[:], attn_bias.broadcast_to([P, D])).then_inc(w_loaded, 16)

            xb = x.rearrange("(t s p j) d -> t s p j d", s=UP, p=P, j=NB)
            xlb = xl_tab.rearrange("(t s p j) d -> t s p j d", s=UP, p=P, j=NB)
            xrb = xr_tab.rearrange("(t s p j) k d -> t s p j k d", s=UP, p=P, j=NB)

            def p_step(b, t, s, lo, hi):
                if lo <= 0 < hi:
                    if not (isinstance(b, int) and b < UP):
                        sp.wait_ge(p_hn, b - (UP - 1))
                        alone(sp, sp_passed)
                    sp.dma_start(px[:, s], xb[bass.ds(t, 1), s].rearrange("a p j d -> (a p) j d")).then_inc(px_loaded[s], 16)
                if lo <= 3 < hi:
                    sp.wait_ge(p_add, b - 2)
                    alone(sp, sp_passed)
                    sp.dma_start(xlb[bass.ds(t - 1, 1), s].rearrange("a p j d -> (a p) j d"),
                                 pf[:, s, :, 0:D]).then_inc(p_stored[s], 16)
                    sp.wait_ge(p_low, b - 2)
                    alone(sp, sp_passed)
                    sp.dma_start(xrb[bass.ds(t - 1, 1), s].rearrange("a p j k d -> (a p) j k d"),
                                 pxr[:, s]).then_inc(p_stored[s], 16)

            batches(sp, p_step, 4)
            for s in range(UP):
                sp.wait_ge(p_stored[s], 32 * (BATCHES // UP))

            def step(w, j, r, lo, hi):
                if lo <= 0 < hi:
                    if not (isinstance(w, int) and w < UN):
                        sp.wait_ge(v_last, done(w, UN))
                        alone(sp, sp_passed)
                        sp.wait_ge(v_diff, done(w, UN))
                        alone(sp, sp_passed)
                        sp.wait_ge(v_dl, done(w, UN))
                        alone(sp, sp_passed)
                        sp.wait_ge(pe_z, done(w, UN, 4, 4))
                        alone(sp, sp_passed)
                    g = sp.value_load(item_i[0:1, 0, bass.ds(w, 1)], min_val=0, max_val=G - 1)
                    sp.dma_start(edg[:, j], edges[:, bass.ds(g, 1)].rearrange("p a k c -> p (a k) c")).then_inc(idx_loaded[j], 16)
                    sp.dma_start(drow[0:CH * H, j, :], dst_row[bass.ds(g, 1)].rearrange("a c e -> (a c) e")).then_inc(idx_loaded[j], 16)
                if lo <= 1 < hi:
                    s = (j - 1) % 2
                    if not (isinstance(w, int) and w < 3):
                        sp.wait_ge(pe_z, done(w, 3, 4, 4))
                        alone(sp, sp_passed)
                    g = sp.value_load(item_i[0:1, 0, bass.ds(w - 1, 1)], min_val=0, max_val=G - 1)
                    base = sp.value_load(item_i[0:1, 1, bass.ds(w - 1, 1)], min_val=0, max_val=N)
                    sp.dma_start(ea[:, s], ea_t[:, bass.ds(g, 1), :].rearrange("p a e -> p (a e)")).then_inc(ea_loaded[s], 16)
                    sp.dma_start(xrw[:, s], xr_tab[bass.ds(base, P)]).then_inc(ea_loaded[s], 16)
                if lo <= 3 < hi:
                    s = (j - 3) % UN
                    if not (isinstance(w, int) and w < UN + 3):
                        sp.wait_ge(v_y1, done(w, UN + 3))
                        alone(sp, sp_passed)
                    base = sp.value_load(item_i[0:1, 1, bass.ds(w - 3, 1)], min_val=0, max_val=N)
                    sp.dma_start(xw[:, s], x[bass.ds(base, P), :]).then_inc(xw_loaded[s], 16)
                if lo <= 6 < hi:
                    base = sp.value_load(item_i[0:1, 1, bass.ds(w - 6, 1)], min_val=0, max_val=N)
                    sp.wait_ge(v_out, done(w, 6))
                    alone(sp, sp_passed)
                    if not (isinstance(w, int) and w == 6):
                        sp.wait_ge(stored, (w - 6) * 16)
                        alone(sp, sp_passed)
                    sp.dma_start(out[bass.ds(base, P), :], ob[:, (j - 6) % 2]).then_inc(stored, 16)

            n_items = items(sp, step, 7)
            sp.wait_ge(stored, n_items * 16)
            alone(sp, sp_passed)

        @block.gpsimd
        def _(pool):
            nc.gpsimd.memset(ones[:], 1.0).then_inc(consts, 1)
            nc.gpsimd.iota(iota_w[:], pattern=[[1, WT]], base=0, channel_multiplier=0,
                           allow_small_or_imprecise_dtypes=True).then_inc(consts, 1)
            nc.gpsimd.iota(iota_p[:], pattern=[[0, 1]], base=0, channel_multiplier=1,
                           allow_small_or_imprecise_dtypes=True).then_inc(consts, 1)
            nc.gpsimd.iota(node_no[:], pattern=[[1, P], [0, CW]], base=0, channel_multiplier=0,
                           allow_small_or_imprecise_dtypes=True).then_inc(consts, 1)
            pool.wait_ge(consts, 4)
            nc.gpsimd.affine_select(out=tri[:], in_=ones[:], compare_op=ALU.is_ge, fill=0.0, base=0,
                                    pattern=[[1, P]], channel_multiplier=-1).then_inc(consts, 1)
            nc.gpsimd.affine_select(out=ident[:], in_=ones[:], compare_op=ALU.is_equal, fill=0.0, base=0,
                                    pattern=[[1, P]], channel_multiplier=-1).then_inc(consts, 1)

            def p_step(b, t, s, lo, hi):
                if lo <= 2 < hi:
                    k = (s - 2) % UP
                    pool.wait_ge(p_hi, b - 1)
                    nc.gpsimd.tensor_tensor(pres[:, k], pf[:, k, :, D:2 * D], pxr[:, k, :, 0], ALU.subtract).then_inc(p_res, 1)
                    pool.wait_ge(p_mid, b - 1)
                    nc.gpsimd.tensor_tensor(pxr[:, k, :, 2], pres[:, k], pxr[:, k, :, 1], ALU.subtract).then_inc(p_low, 1)

            batches(pool, p_step, 3)
            for s in range(UP):
                pool.wait_ge(p_stored[s], 32 * (BATCHES // UP))

            def gathers(w, j, r):
                pool.wait_ge(idx_loaded[j], in_slot(r, j, 0, UN, 32))
                if not (isinstance(w, int) and w < UN):
                    pool.wait_ge(v_msg, done(w, UN))
                alone(pool, pool_passed)
                for c in range(CH):
                    pool.indirect_dma_start(
                        out=gx[:, j, c, :], out_offset=None, in_=xl_tab,
                        in_offset=bass.IndirectOffsetOnAxis(ap=edg[:, j, 0, c:c + 1], axis=0),
                    ).then_inc(gathered[j], 16)

            items(pool, lambda w, j, r, lo, hi: gathers(w, j, r), 1)

        @block.tensor
        def _(pe):
            pe.wait_ge(consts, 6)
            pe.wait_ge(ptab, 1)
            pe.matmul(pch[:, 0:1], tri[:], bnd_f[:, 0:1], start=True, stop=True).then_inc(tab_ps, 1)
            pe.wait_ge(ptab, 2)
            pe.matmul(pch[:, 0:WT], ones[:], tabs[:, 0, :], start=True, stop=True).then_inc(tab_ps, 1)
            pe.matmul(pag[:, 0:WT], ones[:], tabs[:, 1, :], start=True, stop=True).then_inc(tab_ps, 1)
            pe.matmul(pnd[:, 0:WT], ones[:], tabs[:, 2, :], start=True, stop=True).then_inc(tab_ps, 1)
            pe.wait_ge(ptab, 3)
            pe.matmul(pch[:, 0:1], ones[:], bnd_f[:, 0:1], start=True, stop=True).then_inc(tab_ps, 1)

            pe.wait_ge(scaled, 3)
            pe.wait_ge(tables, 1)

            def p_step(b, t, s, lo, hi):
                if lo <= 1 < hi:
                    k = (s - 1) % UP
                    pe.wait_ge(p_hn, b)
                    if not (isinstance(b, int) and b < UP + 1):
                        pe.wait_ge(p_ht, b - UP)
                    for n in range(NB):
                        ins = pe.transpose(p_bank[k][:, n * P:(n + 1) * P], phn[:, k, n], ident[:])
                    ins.then_inc(p_tr, 1)
                    pe.wait_ge(p_ht, b)
                    if not (isinstance(b, int) and b < 2):
                        pe.wait_ge(p_add, b - 1)
                    for n in range(NB):
                        ins = pe.matmul(pz_rows[:, n], pht[:, k, n * P:(n + 1) * P], w_lr[:],
                                        start=n % 2 == 0, stop=n % 2 == 1 or n == NB - 1)
                    ins.then_inc(p_mm, 1)

            batches(pe, p_step, 2)

            def z_start(w, j, q):
                c0, n = GROUPS[q]
                if isinstance(w, int) and w == 1 and q < 2:
                    pe.wait_ge(p_add, BATCHES)
                else:
                    pe.wait_ge(v_leak, group(w, q - 2))
                for k in range(n):
                    pe.matmul(pz[:, q % 2, k], ea[:, (j - 1) % 2, (c0 + k) * P:(c0 + k + 1) * P], w_e[:], start=k == 0, stop=False)
                    pe.matmul(pz[:, q % 2, k], ident[:], gx[:, (j - 1) % UN, c0 + k], start=False, stop=False)

            def z_end(w, j, q):
                c0, n = GROUPS[q]
                for k in range(n):
                    for part in range(3):
                        ins = pe.matmul(pz[:, q % 2, k], mt[:, (j - 1) % 2, (c0 + k) * P:(c0 + k + 1) * P],
                                        xrw[:, (j - 1) % 2, part], start=False, stop=k == n - 1 and part == 2)
                ins.then_inc(pe_z, 1)

            def sums(u, first, last):
                for k in range(first, last):
                    ins = pe.matmul(aggr, m32[:, u, k], msg[:, k * H:(k + 1) * H].rearrange("p a b -> p (a b)"),
                                    start=k == 0, stop=k == CH - 1)
                if last == CH:
                    ins.then_inc(pe_agg, 1)

            def step(w, j, r, lo, hi):
                p, a, b, c, d = (lo <= k < hi for k in range(5))
                v, u = (j - 2) % 2, (j - 3) % 2
                if a:
                    pe.wait_ge(ea_loaded[(j - 1) % 2], in_slot(r, j, 1, 2, 32))
                    pe.wait_ge(gathered[(j - 1) % UN], in_slot(r, j, 1, UN, 16 * CH))
                    z_start(w, j, 0)
                    pe.wait_ge(a_mt, done(w, 1, 2, 2))
                    z_end(w, j, 0)
                if b:
                    pe.wait_ge(v_lg, done(w, 2, 2, 2))
                    pe.transpose(ch_lt[0:CH * H], lg[:, v, :], ident[:]).then_inc(pe_lt, 1)
                if c:
                    pe.wait_ge(v_msg, done(w, 3))
                    pe.wait_ge(a_m32, done(w, 3))
                    sums(u, 0, CH // 2)
                if d:
                    pe.wait_ge(a_hid, done(w, 4))
                    for k in range(4):
                        ins = pe.matmul(pnd[:, 0:D], hid[:, k], w_pr[:, k], start=k == 0, stop=k == 3)
                    ins.then_inc(pe_proj, 1)
                if b:
                    pe.wait_ge(v_scan, done(w, 2))
                    pe.transpose(ch_vt, scan[0:CH * H, :], ident[0:CH * H, 0:CH * H]).then_inc(pe_vt, 1)
                if a:
                    z_start(w, j, 1)
                    z_end(w, j, 1)
                if c:
                    sums(u, CH // 2, CH)
                if a:
                    z_start(w, j, 2)
                    z_end(w, j, 2)
                if b:
                    pe.wait_ge(v_low, done(w, 2))
                    pe.wait_ge(a_hi, done(w, 2))
                    for k in range(CH):
                        o = ch_cand[:, 9 * k:9 * k + 9]
                        pe.matmul(o, m16[:, v, :, k], vs[:, v, k, 0:9], start=True, stop=False, skip_group_check=True)
                        ins = pe.matmul(o[:, 0:H], m16[:, v, :, k], vs[:, v, k, 9:17], start=False, stop=True,
                                        skip_group_check=True)
                    ins.then_inc(pe_sel, 1)
                    if c:
                        pe.wait_ge(v_acc, done(w, 3))
                        pe.wait_ge(v_sel, done(w, 3))
                    pe.matmul(carry, sel[:, u], accs[:, u], start=True, stop=True).then_inc(pe_carry, 1)
                if a:
                    z_start(w, j, 3)
                    z_end(w, j, 3)
                if c:
                    pe.wait_ge(v_hn, done(w, 3))
                    pe.transpose(pnd[:, 0:P], hn[:], ident[:]).then_inc(pe_ht, 1)
                if b:
                    pe.wait_ge(v_mlo, done(w, 2))
                    for k in range(CH):
                        o = ch_sh[:, H * k:H * k + H]
                        for part in range(2):
                            ins = pe.matmul(o, mt[:, v, k * P:(k + 1) * P], ms[:, part * H:(part + 1) * H],
                                            start=part == 0, stop=part == 1, skip_group_check=True)
                    ins.then_inc(pe_sh, 1)
                if p:
                    pe.wait_ge(v_m, done(w, 0))
                    if not (isinstance(w, int) and w < 1):
                        pe.wait_ge(a_mt, done(w, 1, 2, 2))
                    for k in range(CH):
                        ins = pe.transpose(pmt[:, k // 8, (k % 8) * P:(k % 8 + 1) * P], m16[:, j % 2, :, k], ident16[:])
                        if k in (7, CH - 1):
                            ins.then_inc(pe_mt, 1)
                if c:
                    pe.wait_ge(a_hnt, done(w, 3))
                    for k in range(4):
                        ins = pe.matmul(pnd[:, k * P:(k + 1) * P], w_fc[:, k * P:(k + 1) * P], hnt[:],
                                        start=k == 0, stop=k == 3)
                    ins.then_inc(pe_fc, 1)

            items(pe, step, 5)

        @block.scalar
        def _(act):
            nc.scalar.preload_act_table_set("natural_log_exp_and_others")
            act.wait_ge(tables, 1)

            def p_step(b, t, s, lo, hi):
                if lo <= 0 < hi:
                    act.wait_ge(p_stats, NB * b + NB)
                    if not (isinstance(b, int) and b < UP):
                        act.wait_ge(p_hn, b - (UP - 1))
                    nc.scalar.activation(plv[:, s], pmv[:, s, :, 1], ACT.Ln, bias=eps_t[:]).then_inc(p_ln, 1)
                    act.wait_ge(p_ln, b + 1)
                    nc.scalar.activation(prs[:, s], plv[:, s], ACT.Exp, scale=-0.5).then_inc(p_rstd, 1)
                if lo <= 1 < hi:
                    k = (s - 1) % UP
                    act.wait_ge(p_tr, b)
                    if not (isinstance(b, int) and b < UP + 1):
                        act.wait_ge(p_mm, b - UP)
                    nc.scalar.activation(pht[:, k], p_bank[k][:, 0:NB * P], ACT.Copy).then_inc(p_ht, 1)
                if lo <= 2 < hi:
                    k = (s - 2) % UP
                    act.wait_ge(p_add, b - 1)
                    if not (isinstance(b, int) and b < UP + 2):
                        act.wait_ge(p_stored[k], (t + (s - 2) // UP) * 32)
                    nc.scalar.activation(pxr[:, k, :, 0], pf[:, k, :, D:2 * D], ACT.Copy).then_inc(p_hi, 1)
                    act.wait_ge(p_res, b - 1)
                    nc.scalar.activation(pxr[:, k, :, 1], pres[:, k], ACT.Copy).then_inc(p_mid, 1)

            batches(act, p_step, 3)

            def relu(w, q):
                c0, n = GROUPS[q]
                if not (isinstance(w, int) and w < 2):
                    act.wait_ge(v_leak, group(w, q - 4))
                act.wait_ge(pe_z, group(w, q))
                nc.scalar.activation(zr[:, c0:c0 + n], pz[:, q % 2, 0:n], ACT.Relu).then_inc(a_relu, 1)

            def rstd(k, ready, got_ln, got):
                act.wait_ge(*ready)
                nc.scalar.activation(ln_v[:, k:k + 1], mv2[:, k, 1:2], ACT.Ln, bias=eps_t[:]).then_inc(a_ln, 1)
                act.wait_ge(a_ln, got_ln)
                nc.scalar.activation(rs2[:, k:k + 1], ln_v[:, k:k + 1], ACT.Exp, scale=-0.5).then_inc(a_rs, 1)

            def step(w, j, r, lo, hi):
                p, a, b, c, d = (lo <= k < hi for k in range(5))
                n, i, v = j % 2, (j - 1) % 2, (j - 2) % 2
                if a:
                    relu(w, 0)
                if b:
                    act.wait_ge(v_vlast, done(w, 2))
                    nc.scalar.activation(vs[:, v, :, 0:H], vlast[:], ACT.Copy).then_inc(a_hi, 1)
                if d:
                    at = done(w, 4, 2, 2)
                    rstd(1, (v_mvf, done(w, 4)), at, at)
                if a:
                    relu(w, 1)
                    act.wait_ge(v_m, done(w, 1))
                    if c:
                        act.wait_ge(pe_agg, done(w, 3))
                    nc.scalar.activation(m32[:, i], m16[:, i].rearrange("p n c -> p c n")[:, 0:CH], ACT.Copy).then_inc(a_m32, 1)
                    relu(w, 2)
                if c:
                    at = done(w, 3, 1, 2)
                    rstd(0, (v_mv, done(w, 3)), at, at)
                if c:
                    act.wait_ge(pe_ht, done(w, 3))
                    nc.scalar.activation(hnt[:], pnd[:, 0:P], ACT.Copy).then_inc(a_hnt, 1)
                if a:
                    relu(w, 3)
                if p:
                    act.wait_ge(v_diff, done(w, 0))
                    nc.scalar.activation(runf[0:CH * H, n], runf[0:CH * H, n], ACT.Copy, scale=BIG).then_inc(a_runf, 1)
                if b:
                    act.wait_ge(v_farg, done(w, 2))
                    nc.scalar.activation(fac[:, v], farg[:], ACT.Exp).then_inc(a_fac, 1)
                if p:
                    for k, (c0, m) in enumerate(HALVES):
                        act.wait_ge(pe_mt, w * 2 + (k + 1))
                        nc.scalar.activation(mt[:, n, c0 * P:(c0 + m) * P], pmt[:, k, 0:m * P],
                                             ACT.Copy).then_inc(a_mt, 1)
                if b:
                    act.wait_ge(v_dmin, done(w, 2))
                    if c:
                        act.wait_ge(pe_agg, done(w, 3))
                    nc.scalar.activation(msg[:, :, HC], dmin[:], ACT.Exp).then_inc(a_exp, 1)
                if c:
                    act.wait_ge(pe_fc, done(w, 3))
                    nc.scalar.activation(hid[:].rearrange("p a n -> p (a n)"), pnd[:], ACT.Relu).then_inc(a_hid, 1)

            items(act, step, 5)

        @block.vector
        def _(dve):
            V = nc.vector
            dve.wait_ge(w_loaded, 16 * LOADS)
            dve.wait_ge(consts, 6)
            t = [0]

            def link(ins):
                t[0] += 1
                ins.then_inc(scaled_t, 1)
                dve.wait_ge(scaled_t, t[0])

            link(V.tensor_tensor(bnd_d[:], bnd[:, 1:2], bnd[:, 0:1], ALU.subtract))
            link(V.tensor_scalar(bnd_d[:], bnd_d[:], 7, None, ALU.arith_shift_right))
            V.tensor_scalar(bnd_f[:, 0:1], bnd_d[:], 1.0, None, ALU.add).then_inc(ptab, 1)
            dve.wait_ge(tab_ps, 1)
            link(V.tensor_copy(bnd_f[:, 1:2], pch[:, 0:1]))
            link(V.tensor_tensor(bnd_f[:, 2:3], bnd_f[:, 1:2], bnd_f[:, 0:1], ALU.subtract))
            link(V.tensor_copy(bnd_f[:, 3:4], bnd[:, 0:1]))
            link(V.scalar_tensor_tensor(bnd_f[:, 4:5], bnd_f[:, 2:3], -float(P), bnd_f[:, 3:4], ALU.mult, ALU.add))
            link(V.tensor_scalar(tabs[:, 3, :], iota_w[:], bnd_f[:, 2:3], None, ALU.is_ge))
            link(V.scalar_tensor_tensor(tabs[:, 1, :], iota_w[:], bnd_f[:, 1:2], tabs[:, 3, :], ALU.is_lt, ALU.mult))
            link(V.tensor_scalar(tabs[:, 3, :], iota_w[:], float(P), bnd_f[:, 4:5], ALU.mult, ALU.add))
            link(V.tensor_tensor(tabs[:, 0, :], tabs[:, 3, :], tabs[:, 1, :], ALU.mult))
            V.tensor_scalar(tabs[:, 2, :], iota_w[:], bnd_f[:, 1:2], None, ALU.is_ge).then_inc(ptab, 1)
            dve.wait_ge(tab_ps, 4)
            link(V.tensor_scalar(tabs[:, 3, :], pag[:, 0:WT], -float(N), float(N), ALU.mult, ALU.add))
            link(V.tensor_tensor(base_f[:], tabs[:, 3, :], pch[:, 0:WT], ALU.add))
            link(V.tensor_scalar(item_i[:, 0, :], pnd[:, 0:WT], float(G - 1), None, ALU.min))
            link(V.tensor_copy(item_i[:, 1, :], base_f[:]))
            link(V.memset(delta_f[:], 0.0))
            V.tensor_tensor(delta_f[:, 0:WT - 1], base_f[:, 1:WT], base_f[:, 0:WT - 1], ALU.subtract).then_inc(ptab, 1)
            dve.wait_ge(tab_ps, 5)
            link(V.tensor_copy(bnd_f[:, 5:6], pch[:, 0:1]))
            link(V.tensor_scalar(cnt_f[:, 0, :], iota_w[:, 0:P], float(UN), bnd_f[:, 5:6], ALU.mult, ALU.is_lt))
            link(V.tensor_reduce(bnd_f[:, 6:7], cnt_f[:, 0, :], AX.X, ALU.add))
            link(V.tensor_scalar(more_i[:], bnd_f[:, 6:7], float(-(G // UN)), None, ALU.add))
            V.tensor_scalar(w_lr[:], w_lr[:], ln1[:], None, ALU.mult).then_inc(scaled, 1)
            V.tensor_scalar(w_fc[:], w_fc[:], ln2[:], None, ALU.mult).then_inc(scaled, 1)
            V.tensor_copy(ident16[:], ident[:]).then_inc(scaled, 1)
            link(V.tensor_scalar(att_b[:], att_b[:], 1.0 - SLOPE, None, ALU.mult))
            link(V.memset(sel[:], 0.0))
            link(V.memset(accs[:], 0.0))
            link(V.memset(accs[:, :, AW + H:AW + H + 1], 1.0))
            link(V.memset(runf[:], 0.0))
            link(V.memset(vs[:], 0.0))
            V.memset(eps_t[:], EPS).then_inc(tables, 1)
            dve.wait_ge(tables, 1)

            def p_step(b, t, s, lo, hi):
                if lo <= 0 < hi:
                    dve.wait_ge(px_loaded[s], 16 * t + 16)
                    for n in range(NB):
                        ins = V.bn_stats(pst[:, s, n], px[:, s, n])
                    ins.then_inc(p_bn, 1)
                if lo <= 1 < hi:
                    k = (s - 1) % UP
                    dve.wait_ge(p_rstd, b)
                    if not (isinstance(b, int) and b < UP + 1):
                        dve.wait_ge(p_tr, b - UP)
                    for n in range(NB):
                        ins = V.tensor_scalar(phn[:, k, n], px[:, k, n], pmv[:, k, n, 0:1], prs[:, k, n:n + 1],
                                              ALU.subtract, ALU.mult)
                    ins.then_inc(p_hn, 1)
                if lo <= 0 < hi:
                    dve.wait_ge(p_bn, b + 1)
                    alone(dve, dve_passed)
                    for n in range(NB):
                        V.bn_aggr(pmv[:, s, n], pst[:, s, n]).then_inc(p_stats, 1)
                if lo <= 2 < hi:
                    k = (s - 2) % UP
                    if not (isinstance(b, int) and b < UP + 2):
                        dve.wait_ge(p_stored[k], (t + (s - 2) // UP) * 32)
                    dve.wait_ge(p_mm, b - 1)
                    V.tensor_tensor(pf[:, k], pz_rows[:, 0:NB], b_lr[:].unsqueeze(1).broadcast_to([P, NB, 2 * D]),
                                    ALU.add).then_inc(p_add, 1)

            batches(dve, p_step, 3)

            def leaky(w, q):
                c0, n = GROUPS[q]
                dve.wait_ge(a_relu, group(w, q))
                V.scalar_tensor_tensor(zl[:, c0:c0 + n], pz[:, q % 2, 0:n], SLOPE / (1.0 - SLOPE), zr[:, c0:c0 + n],
                                       ALU.mult, ALU.add).then_inc(v_leak, 1)

            def times_att(w, q):
                c0, n = GROUPS[q]
                dve.wait_ge(v_leak, group(w, q))
                V.tensor_tensor(zl[:, c0:c0 + n], zl[:, c0:c0 + n], att_b[:].unsqueeze(1).broadcast_to([P, n, D]),
                                ALU.mult).then_inc(v_att, 1)

            def logits(w, j, half):
                c0, n = HALVES[half]
                dve.wait_ge(v_att, group(w, 2 * half + 1))
                V.tensor_reduce(lg[:, (j - 1) % 2, c0 * H:(c0 + n) * H],
                                zl[:, c0:c0 + n].rearrange("p c (h k) -> p (c h) k", k=HC), AX.X, ALU.add).then_inc(v_lg, 1)

            def step(w, j, r, lo, hi):
                p, a, b, c, d = (lo <= k < hi for k in range(5))
                n, v, u, y = j % 2, (j - 2) % 2, (j - 3) % 2, (j - 4) % 2
                xu = (j - 3) % UN
                if b:
                    dve.wait_ge(pe_lt, done(w, 2))
                    dve.wait_ge(a_runf, done(w, 2))
                    V.tensor_tensor_scan(scan[0:CH * H, :], runf[0:CH * H, v], ch_lt[0:CH * H], -BIG,
                                         ALU.add, ALU.max).then_inc(v_scan, 1)
                if a:
                    leaky(w, 0)
                if c:
                    dve.wait_ge(xw_loaded[xu], in_slot(r, j, 3, UN, 16))
                    V.tensor_tensor(xab[:], xw[:, xu], a_bias[:], ALU.add).then_inc(v_xab, 1)
                if a:
                    times_att(w, 0)
                if c:
                    V.tensor_scalar(sel[:, u, 0:1], iota_p[:], delta_f[:, bass.ds(w - 3, 1)], None,
                                    ALU.is_equal).then_inc(v_sel, 1)
                if d:
                    dve.wait_ge(v_y1, done(w, 4))
                    dve.wait_ge(pe_proj, done(w, 4))
                    V.tensor_tensor(y1[:, y], y1[:, y], pnd[:, 0:D], ALU.add).then_inc(v_y, 1)
                if b:
                    dve.wait_ge(pe_vt, done(w, 2))
                    V.tensor_tensor(vlast[:], ch_vt.rearrange("p (c h) -> p c h", h=H),
                                    vs[:, v, :, H:H + 1].broadcast_to([P, CH, H]), ALU.mult).then_inc(v_vlast, 1)
                if d:
                    dve.wait_ge(v_y, done(w, 4))
                    V.bn_stats(st2[:, 1], y1[:, y]).then_inc(v_stf, 1)
                    dve.wait_ge(v_stf, done(w, 4))
                    alone(dve, dve_passed)
                    V.bn_aggr(mv2[:, 1], st2[:, 1]).then_inc(v_mvf, 1)
                if b:
                    dve.wait_ge(a_hi, done(w, 2))
                    V.tensor_tensor(vs[:, v, :, H + 1:2 * H + 1], vlast[:], vs[:, v, :, 0:H], ALU.subtract).then_inc(v_low, 1)
                if a:
                    leaky(w, 1)
                    times_att(w, 1)
                if c:
                    dve.wait_ge(pe_agg, done(w, 3))
                    dve.wait_ge(v_tmp, done(w, 3))
                    V.tensor_tensor(accs[:, u, 0:AW], tmpa[:], aggr, ALU.add).then_inc(v_acc, 1)
                if a:
                    logits(w, j, 0)
                if c:
                    dve.wait_ge(v_acc, done(w, 3))
                    V.tensor_scalar(rden[:, 0], accs[:, u, HC:AW:MS], 1e-30, None, ALU.max).then_inc(v_den, 1)
                if d:
                    dve.wait_ge(a_rs, done(w, 4, 2, 2))
                    if not (isinstance(w, int) and w < 6):
                        dve.wait_ge(stored, (w - 5) * 16)
                    V.tensor_scalar(ob[:, y], y1[:, y], mv2[:, 1, 0:1], rs2[:, 1:2], ALU.subtract, ALU.mult).then_inc(v_out, 1)
                if c:
                    dve.wait_ge(v_den, done(w, 3))
                    V.reciprocal(rden[:, 1], rden[:, 0]).then_inc(v_rden, 1)
                    dve.wait_ge(v_rden, done(w, 3))
                    V.tensor_tensor(attn[:].rearrange("p (h k) -> p h k", k=HC),
                                    accs[:, u, 0:AW].rearrange("p (h k) -> p h k", k=MS)[:, :, 0:HC],
                                    rden[:, 1].unsqueeze(2).broadcast_to([P, H, HC]), ALU.mult).then_inc(v_attn, 1)
                if b:
                    dve.wait_ge(pe_sel, done(w, 2))
                    V.tensor_scalar(pen[:], ch_cand.rearrange("p (c k) -> p c k", k=9)[:, :, 8], -1.0, BIG,
                                    ALU.add, ALU.mult).then_inc(v_pen, 1)
                if c:
                    dve.wait_ge(v_attn, done(w, 3))
                    V.tensor_tensor(x1[:, u], attn[:], xab[:], ALU.add).then_inc(v_x1, 1)
                if b:
                    dve.wait_ge(v_pen, done(w, 2))
                    V.tensor_tensor(cand[:], ch_cand.rearrange("p (c k) -> p c k", k=9)[:, :, 0:8],
                                    pen[:].unsqueeze(2).broadcast_to([P, CH, H]), ALU.add).then_inc(v_cand, 1)
                if c:
                    dve.wait_ge(v_x1, done(w, 3))
                    V.bn_stats(st2[:, 0], x1[:, u]).then_inc(v_st, 1)
                if b:
                    dve.wait_ge(pe_carry, done(w, 2))
                    V.tensor_scalar(pen2[:], carry[:, AW + H:AW + H + 1], -1.0, BIG, ALU.add, ALU.mult).then_inc(v_pen2, 1)
                    dve.wait_ge(v_cand, done(w, 2))
                    V.tensor_reduce(mblk[:], cand[:].rearrange("p c h -> p h c"), AX.X, ALU.max).then_inc(v_mblk, 1)
                if c:
                    dve.wait_ge(v_st, done(w, 3))
                    alone(dve, dve_passed)
                    V.bn_aggr(mv2[:, 0], st2[:, 0]).then_inc(v_mv, 1)
                if a:
                    leaky(w, 2)
                if b:
                    dve.wait_ge(v_mblk, done(w, 2))
                    dve.wait_ge(v_pen2, done(w, 2))
                    V.scalar_tensor_tensor(accs[:, v, AW:AW + H], carry[:, AW:AW + H], pen2[:], mblk[:],
                                           ALU.add, ALU.max).then_inc(v_max, 1)
                if a:
                    times_att(w, 2)
                if b:
                    dve.wait_ge(v_max, done(w, 2))
                    V.tensor_copy(ms[:, 0:H], accs[:, v, AW:AW + H]).then_inc(v_mhi, 1)
                    V.scalar_tensor_tensor(farg[:], carry[:, AW:AW + H], pen2[:], accs[:, v, AW:AW + H],
                                           ALU.add, ALU.subtract).then_inc(v_farg, 1)
                if c:
                    dve.wait_ge(a_rs, done(w, 3, 1, 2))
                    V.tensor_scalar(hn[:], x1[:, u], mv2[:, 0, 0:1], rs2[:, 0:1], ALU.subtract, ALU.mult).then_inc(v_hn, 1)
                if b:
                    dve.wait_ge(v_mhi, done(w, 2))
                    V.tensor_tensor(ms[:, H:2 * H], accs[:, v, AW:AW + H], ms[:, 0:H], ALU.subtract).then_inc(v_mlo, 1)
                if c:
                    V.tensor_tensor(y1[:, u], x1[:, u], xw[:, xu], ALU.add).then_inc(v_y1, 1)
                if p:
                    dve.wait_ge(idx_loaded[j], in_slot(r, j, 0, UN, 32))
                    V.tensor_scalar(dl[:, n], edg[:, j, 1], base_f[:, bass.ds(w, 1)], None, ALU.subtract).then_inc(v_dl, 1)
                    V.tensor_tensor(vs[:, n, :, H], edg[:, j, 1, 0:CH], edg[:, j, 2, 0:CH], ALU.not_equal).then_inc(v_last, 1)
                    V.tensor_tensor(runf[0:CH * H, n, 1:P], drow[0:CH * H, j, 0:P - 1], drow[0:CH * H, j, 1:P],
                                    ALU.subtract).then_inc(v_diff, 1)
                    dve.wait_ge(v_dl, done(w, 0))
                    V.tensor_tensor(m16[:, n], dl[:, n].unsqueeze(1).broadcast_to([P, P, CW]), node_no[:],
                                    ALU.is_equal).then_inc(v_m, 1)
                if a:
                    leaky(w, 3)
                if b:
                    dve.wait_ge(pe_sh, done(w, 2))
                    V.tensor_tensor(dlt[:], lg[:, v], ch_sh, ALU.subtract).then_inc(v_dlt, 1)
                if a:
                    times_att(w, 3)
                if b:
                    dve.wait_ge(v_dlt, done(w, 2))
                    V.tensor_scalar(dmin[:], dlt[:], 0.0, None, ALU.min).then_inc(v_dmin, 1)
                    dve.wait_ge(a_fac, done(w, 2))
                    V.tensor_tensor(tmpa[:].rearrange("p (h k) -> p h k", k=MS),
                                    carry[:, 0:AW].rearrange("p (h k) -> p h k", k=MS),
                                    fac[:, v].unsqueeze(2).broadcast_to([P, H, MS]), ALU.mult).then_inc(v_tmp, 1)
                if a:
                    logits(w, j, 1)
                if b:
                    dve.wait_ge(a_exp, done(w, 2))
                    V.tensor_tensor(msg[:, :, 0:HC], gx[:, (j - 2) % UN].rearrange("p c (h k) -> p (c h) k", k=HC),
                                    msg[:, :, HC:MS].broadcast_to([P, CH * H, HC]), ALU.mult).then_inc(v_msg, 1)

            items(dve, step, 5)


def kernel(x, src, dst, edge_attr_128, L0_gnn_ln1_w, L0_gnn_lin_l_w, L0_gnn_lin_l_b, L0_gnn_lin_r_w,
           L0_gnn_lin_r_b, L0_gnn_lin_edge_w, L0_gnn_att, L0_gnn_attn_bias, L0_gnn_ln2_w, L0_gnn_fc_w,
           L0_gnn_proj_w):
    import numpy as np
    import concourse.bacc as bacc
    from concourse.bass_utils import run_bass_kernel_spmd

    a = lambda v: np.asarray(v)
    xs = np.zeros((NP, D), np.float32)
    xs[:N] = a(x)
    ea_t = np.zeros((D, EP), np.float32)
    ea_t[:, :E] = a(edge_attr_128).T
    src_p, dst_p = np.zeros(EP, np.int32), np.full(EP, -1, np.int32)
    src_p[:E], dst_p[:E] = a(src), a(dst)
    edges = np.full((P, G, 3, CW), -1, np.int32)
    edges[:, :, 0, :CH] = src_p.reshape(G, CH, P).transpose(2, 0, 1)
    edges[:, :, 0, CH:] = 0
    edges[:, :, 1, :CH] = dst_p.reshape(G, CH, P).transpose(2, 0, 1)
    edges[:-1, :, 2, :CH] = edges[1:, :, 1, :CH]
    edges[-1, :, 2, :] = -2
    dst_row = np.repeat(dst_p.reshape(G, CH, P), H, axis=1)
    bounds = np.zeros((P, 2), np.int32)
    bounds[:, 1] = -P
    ends = dst_p[EG - 1:E:EG][:G - 1]
    bounds[1:G, 0] = ends
    bounds[:G - 1, 1] = ends
    bounds[G - 1, 1] = N - 1
    arrays = {
        "x": xs,
        "ea_t": ea_t.reshape(D, G, EG),
        "edges": edges,
        "dst_row": dst_row,
        "bounds": bounds,
        "ln1_w": a(L0_gnn_ln1_w).reshape(D, 1),
        "wlr_t": np.concatenate([a(L0_gnn_lin_l_w).T, a(L0_gnn_lin_r_w).T], 1),
        "blr": np.concatenate([a(L0_gnn_lin_l_b), a(L0_gnn_lin_r_b)]).reshape(1, 2 * D),
        "we_t": a(L0_gnn_lin_edge_w).T,
        "att": a(L0_gnn_att).reshape(1, D),
        "attn_bias": a(L0_gnn_attn_bias).reshape(1, D),
        "ln2_w": a(L0_gnn_ln2_w).reshape(D, 1),
        "fc_t": a(L0_gnn_fc_w).T,
        "proj_t": a(L0_gnn_proj_w).T.reshape(4, P, D).transpose(1, 0, 2),
    }
    arrays = {k: np.ascontiguousarray(v) for k, v in arrays.items()}
    nc = bacc.Bacc("TRN2", target_bir_lowering=False, num_devices=1)
    args = {k: nc.dram_tensor(f"{k}_in", v.shape, mybir.dt.from_np(v.dtype), kind="ExternalInput").ap()
            for k, v in arrays.items()}
    out = nc.dram_tensor("out_rows", (NP, D), F32, kind="ExternalOutput").ap()
    gnn_kernel(nc, out=out, **args)
    r = run_bass_kernel_spmd(nc, [{f"{k}_in": v for k, v in arrays.items()}], core_ids=[0])
    return r.results[0]["out_rows"][:N]
```

```python
from contextlib import ExitStack

import concourse.bass as bass
from concourse import mybir

P = 128
N, E, D, H = 12500, 200000, 128, 8
HC = D // H
CH = 14
EG = CH * P
G = -(-E // EG)
EP = G * EG
CW = CH + CH % 2
GROUPS = [(0, 4), (4, 4), (8, 2), (10, 4)]
SUMMED = (3,)
HALVES = [(0, 8), (8, CH - 8)]
UN = 4
NB = 3
UP = 3
BATCHES = 33
NP = BATCHES * NB * P
WT = 216
HID = 4 * D
MAX_ROUNDS = -(-(G + N // P) // UN)
MS = HC + 1
AW = H * MS
BIG = 1.0e30
EPS = 1e-05
SLOPE = 0.2
assert G <= P and G % UN == 0 and G // UN > 2 and NP >= N + P and MAX_ROUNDS * UN < WT

ALU = mybir.AluOpType
ACT = mybir.ActivationFunctionType
AX = mybir.AxisListType
F32 = mybir.dt.float32
BF16 = mybir.dt.bfloat16
I32 = mybir.dt.int32


def gnn_kernel(nc, x, ea_t, edges, dst_row, bounds, ln1_w, wlr_t, blr, we_t, att, attn_bias,
               ln2_w, fc_t, proj_t, out):
    xl_tab = nc.dram_tensor("xl_tab", (NP, D), F32, kind="Internal").ap()
    xr_tab = nc.dram_tensor("xr_tab", (NP, 3, D), BF16, kind="Internal").ap()

    with ExitStack() as ctx:
        def sb(name, shape, dt=F32):
            return ctx.enter_context(nc.sbuf_tensor(name, shape, dt))

        def ps(name, shape, dt=F32):
            return ctx.enter_context(nc.psum_tensor(name, shape, dt))

        def sem(name):
            return ctx.enter_context(nc.semaphore(name))

        def sems(name, n):
            return [sem(f"{name}{k}") for k in range(n)]

        ident = sb("ident", [P, P])
        ident16 = sb("ident16", [P, P], BF16)
        ones = sb("ones", [P, P])
        tri = sb("tri", [P, P])
        iota_p = sb("iota_p", [P, 1])
        iota_w = sb("iota_w", [P, WT])
        node_no = sb("node_no", [P, P, CW], BF16)
        w_lr = sb("w_lr", [P, 2 * D])
        b_lr = sb("b_lr", [P, 2 * D])
        w_e = sb("w_e", [P, D])
        w_fc = sb("w_fc", [P, HID])
        w_pr = sb("w_pr", [P, 4, D])
        att_b = sb("att_b", [P, D])
        a_bias = sb("a_bias", [P, D])
        ln1 = sb("ln1", [P, 1])
        ln2 = sb("ln2", [P, 1])
        bnd = sb("bnd", [P, 2], I32)
        bnd_d = sb("bnd_d", [P, 1], I32)
        bnd_f = sb("bnd_f", [P, 8])
        tabs = sb("tabs", [P, 4, WT])
        base_f = sb("base_f", [P, WT])
        minus_base = sb("minus_base", [P, WT])
        minus_delta = sb("minus_delta", [P, WT])
        apart = sb("apart", [P, 1])
        item_i = sb("item_i", [P, 2, WT], I32)
        cnt_f = sb("cnt_f", [P, 2, P])
        more_i = sb("more_i", [P, 1], I32)
        px = sb("px", [P, UP, NB, D])
        pst = sb("pst", [P, UP, NB, 6])
        pmv = sb("pmv", [P, UP, NB, 2])
        plv = sb("plv", [P, UP, NB])
        prs = sb("prs", [P, UP, NB])
        eps_t = sb("eps_t", [P, 1])
        phn = sb("phn", [P, UP, NB, D])
        pht = sb("pht", [P, UP, NB * P])
        pf = sb("pf", [P, UP, NB, 2 * D])
        pres = sb("pres", [P, UP, NB, D])
        pxr = sb("pxr", [P, UP, NB, 3, D], BF16)
        edg = sb("edg", [P, UN, 3, CW], I32)
        drow = sb("drow", [P, UN, P], I32)
        ea = sb("ea", [P, 2, EG])
        gx = sb("gx", [P, UN, CH, D])
        xrw = sb("xrw", [P, 2, 3, D], BF16)
        xw = sb("xw", [P, UN, D])
        dl = sb("dl", [P, 2, CW], BF16)
        runf = sb("runf", [P, 2, P])
        m16 = sb("m16", [P, UN, P, CW], BF16)
        m32 = sb("m32", [P, 2, CH, P])
        mt = sb("mt", [P, UN, CH * P], BF16)
        zr = sb("zr", [P, CH, D])
        zl = sb("zl", [P, CH, D])
        lg = sb("lg", [P, 2, CH * H])
        scan = sb("scan", [P, P])
        vlast = sb("vlast", [P, CH, H])
        vs = sb("vs", [P, UN, CH, 2 * H + 1], BF16)
        pen = sb("pen", [P, CH])
        cand_low = sb("cand_low", [P, CH, H])
        cand = sb("cand", [P, CH, H])
        mblk = sb("mblk", [P, H])
        pen2 = sb("pen2", [P, 1])
        ms = sb("ms", [P, 2 * H], BF16)
        farg = sb("farg", [P, H])
        fac = sb("fac", [P, 2, H])
        dlt_hi = sb("dlt_hi", [P, CH, H])
        dlt = sb("dlt", [P, CH * H])
        dmin = sb("dmin", [P, CH * H])
        msg = sb("msg", [P, CH * H, MS])
        accs = sb("accs", [P, 2, AW + H + 1])
        tmpa = sb("tmpa", [P, AW])
        sel = sb("sel", [P, 2, P])
        rden = sb("rden", [P, 2, H])
        attn = sb("attn", [P, D])
        xab = sb("xab", [P, D])
        x1 = sb("x1", [P, 2, D])
        y1 = sb("y1", [P, 2, D])
        st2 = sb("st2", [P, 2, 6])
        mv2 = sb("mv2", [P, 2, 2])
        ln_v = sb("ln_v", [P, 2])
        rs2 = sb("rs2", [P, 2])
        neg2 = sb("neg2", [P, 2])
        off2 = sb("off2", [P, 2])
        hn = sb("hn", [P, D])
        hnt = sb("hnt", [P, P])
        hid = sb("hid", [P, 4, P])
        ob = sb("ob", [P, 2, D])

        pz = ps("pz", [P, 2, 4, D])
        pmt = ps("pmt", [P, 2, 8 * P], BF16)
        pch = ps("pch", [P, 512])
        pag = ps("pag", [P, 512])
        pcy = ps("pcy", [P, 512])
        pnd = ps("pnd", [P, 512])
        ch_lt, ch_vt = pch[:, 0:P], pch[:, P:P + CH * H]
        ch_sh = pch[:, 0:CH * 2 * H].rearrange("p (c k) -> p c k", k=2 * H)
        ch_cand = pch[:, 240:240 + CH * (2 * H + 1)].rearrange("p (c k) -> p c k", k=2 * H + 1)
        carry, aggr, mlp_out = pcy[:, 0:AW + H + 1], pag[:, 0:AW], pag[:, 256:256 + D]

        p_bank = (pch, pag, pcy)
        pz_rows = pz[:].rearrange("p b (t a) d -> p (b t) (a d)", a=2)

        bounds_loaded = sem("bounds_loaded")
        w_loaded = sem("w_loaded")
        consts = sem("consts")
        scaled = sem("scaled")
        table_steps = sem("table_steps")
        tables = sem("tables")
        tab_ps = sem("tab_ps")
        ptab = sem("ptab")
        px_loaded = sems("px_loaded", UP)
        p_stats = sem("p_stats")
        p_bn = sem("p_bn")
        p_rstd = sem("p_rstd")
        p_ln = sem("p_ln")
        p_hn = sem("p_hn")
        p_tr = sem("p_tr")
        p_ht = sem("p_ht")
        p_mm = sem("p_mm")
        p_add = sem("p_add")
        p_hi = sem("p_hi")
        p_res = sem("p_res")
        p_mid = sem("p_mid")
        p_low = sem("p_low")
        p_stored = sems("p_stored", UP)
        idx_loaded = sems("idx_loaded", UN)
        ea_loaded = sems("ea_loaded", 2)
        xw_loaded = sems("xw_loaded", UN)
        gathered = sems("gathered", UN)
        stored = sem("stored")
        pe_lt = sem("pe_lt"); pe_z = sem("pe_z"); pe_mt = sem("pe_mt"); pe_carry = sem("pe_carry")
        pe_vt = sem("pe_vt"); pe_sel = sem("pe_sel"); pe_sh = sem("pe_sh"); pe_ht = sem("pe_ht")
        pe_fc = sem("pe_fc"); pe_agg = sem("pe_agg"); pe_proj = sem("pe_proj")
        a_runf = sem("a_runf"); a_mt = sem("a_mt"); a_hi = sem("a_hi"); a_relu = sem("a_relu")
        a_m32 = sem("a_m32"); a_hnt = sem("a_hnt")
        a_hid = sem("a_hid"); a_fac = sem("a_fac"); a_exp = sem("a_exp")
        a_ln = sems("a_ln", 2); a_rs = sems("a_rs", 2); a_neg = sems("a_neg", 2); a_off = sems("a_off", 2)
        a_dl = sem("a_dl"); a_apart = sem("a_apart"); a_sel = sem("a_sel"); a_hn = sem("a_hn"); a_out = sem("a_out")
        v_last = sem("v_last"); v_diff = sem("v_diff"); v_m = sem("v_m")
        v_scan = sem("v_scan"); v_tmp = sem("v_tmp"); v_acc = sem("v_acc"); v_vlast = sem("v_vlast")
        v_low = sem("v_low"); v_leak = sem("v_leak"); v_att = sem("v_att"); v_lg = sem("v_lg")
        v_pen = sem("v_pen"); v_cand = sem("v_cand"); v_clow = sem("v_clow"); v_mblk = sem("v_mblk"); v_max = sem("v_max")
        v_farg = sem("v_farg"); v_mhi = sem("v_mhi"); v_mlo = sem("v_mlo"); v_dlt = sem("v_dlt"); v_dhi = sem("v_dhi")
        v_dmin = sem("v_dmin"); v_msg = sem("v_msg"); v_den = sem("v_den"); v_rden = sem("v_rden")
        v_attn = sem("v_attn"); v_x1 = sem("v_x1"); v_st = sem("v_st")
        v_mv = sem("v_mv"); v_y1 = sem("v_y1")
        v_y = sem("v_y"); v_sum = sem("v_sum"); v_stf = sem("v_stf"); v_mvf = sem("v_mvf")
        v_pen2 = sem("v_pen2")

        LOADS = 9
        PEEL = 2 * UN

        def items(eng, body, depth):
            eng.wait_ge(tables, 1)
            more = eng.value_load(more_i[0:1, 0:1], min_val=0, max_val=MAX_ROUNDS - G // UN)
            n_rounds = eng.snap(more + G // UN)
            n_items = eng.snap(n_rounds * UN)
            for w in range(PEEL):
                body(w, w % UN, w // UN, 0, min(depth, w + 1))
            with eng.Fori(PEEL // UN, n_rounds) as r:
                w0 = eng.snap(r * UN)
                for j in range(UN):
                    body(w0 + j, j, r, 0, depth)
            for j in range(depth - 1):
                body(n_items + j, j % UN, n_rounds + j // UN, j + 1, depth)
            return n_items

        def done(w, back, n=1, per=1):
            return w * per + (n - back * per)

        def in_slot(r, j, back, slots, per):
            return r * (per * UN // slots) + ((j - back) // slots + 1) * per

        def batches(eng, body, depth):
            for b in range(2 * UP):
                body(b, b // UP, b % UP, 0, min(depth, b + 1))
            with eng.Fori(2, BATCHES // UP) as t:
                b0 = eng.snap(t * UP)
                for s in range(UP):
                    body(b0 + s, t, s, 0, depth)
            for s in range(depth - 1):
                body(BATCHES + s, BATCHES // UP, s, s + 1, depth)

        def group(w, q):
            return w * 4 + (q - 3)

        sp_passed, pool_passed, dve_passed = sem("sp_passed"), sem("pool_passed"), sem("dve_passed")

        def alone(eng, passed):
            eng.sem_inc(passed, 1)

        block = ctx.enter_context(nc.Block())

        @block.sync
        def _(sp):
            sp.dma_start(bnd[:], bounds).then_inc(bounds_loaded, 16)
            sp.dma_start(w_lr[:], wlr_t).then_inc(w_loaded, 16)
            sp.dma_start(b_lr[:], blr.broadcast_to([P, 2 * D])).then_inc(w_loaded, 16)
            sp.dma_start(ln1[:], ln1_w).then_inc(w_loaded, 16)
            sp.dma_start(ln2[:], ln2_w).then_inc(w_loaded, 16)
            sp.dma_start(w_e[:], we_t).then_inc(w_loaded, 16)
            sp.dma_start(w_fc[:], fc_t).then_inc(w_loaded, 16)
            sp.dma_start(w_pr[:], proj_t).then_inc(w_loaded, 16)
            sp.dma_start(att_b[:], att.broadcast_to([P, D])).then_inc(w_loaded, 16)
            sp.dma_start(a_bias[:], attn_bias.broadcast_to([P, D])).then_inc(w_loaded, 16)

            xb = x.rearrange("(t s p j) d -> t s p j d", s=UP, p=P, j=NB)
            xlb = xl_tab.rearrange("(t s p j) d -> t s p j d", s=UP, p=P, j=NB)
            xrb = xr_tab.rearrange("(t s p j) k d -> t s p j k d", s=UP, p=P, j=NB)

            def p_step(b, t, s, lo, hi):
                if lo <= 0 < hi:
                    if not (isinstance(b, int) and b < UP):
                        sp.wait_ge(p_hn, b - (UP - 1))
                        alone(sp, sp_passed)
                    sp.dma_start(px[:, s], xb[bass.ds(t, 1), s].rearrange("a p j d -> (a p) j d")).then_inc(px_loaded[s], 16)
                if lo <= 4 < hi:
                    k, at = (s - 4) % UP, t + (s - 4) // UP
                    sp.wait_ge(p_add, b - 3)
                    alone(sp, sp_passed)
                    sp.dma_start(xlb[bass.ds(at, 1), k].rearrange("a p j d -> (a p) j d"),
                                 pf[:, k, :, 0:D]).then_inc(p_stored[k], 16)
                    sp.wait_ge(p_low, b - 3)
                    alone(sp, sp_passed)
                    sp.dma_start(xrb[bass.ds(at, 1), k].rearrange("a p j k d -> (a p) j k d"),
                                 pxr[:, k]).then_inc(p_stored[k], 16)

            batches(sp, p_step, 5)
            for s in range(UP):
                sp.wait_ge(p_stored[s], 32 * (BATCHES // UP))

            def step(w, j, r, lo, hi):
                if lo <= 0 < hi:
                    if not (isinstance(w, int) and w < UN):
                        sp.wait_ge(v_last, done(w, UN))
                        alone(sp, sp_passed)
                        sp.wait_ge(v_diff, done(w, UN))
                        alone(sp, sp_passed)
                        sp.wait_ge(a_dl, done(w, UN))
                        alone(sp, sp_passed)
                        sp.wait_ge(pe_z, done(w, UN, 4, 4))
                        alone(sp, sp_passed)
                    g = sp.value_load(item_i[0:1, 0, bass.ds(w, 1)], min_val=0, max_val=G - 1)
                    sp.dma_start(edg[:, j], edges[:, bass.ds(g, 1)].rearrange("p a k c -> p (a k) c")).then_inc(idx_loaded[j], 16)
                    sp.dma_start(drow[0:CH * H, j, :], dst_row[bass.ds(g, 1)].rearrange("a c e -> (a c) e")).then_inc(idx_loaded[j], 16)
                if lo <= 1 < hi:
                    s = (j - 1) % 2
                    if not (isinstance(w, int) and w < 3):
                        sp.wait_ge(pe_z, done(w, 3, 4, 4))
                        alone(sp, sp_passed)
                    g = sp.value_load(item_i[0:1, 0, bass.ds(w - 1, 1)], min_val=0, max_val=G - 1)
                    base = sp.value_load(item_i[0:1, 1, bass.ds(w - 1, 1)], min_val=0, max_val=N)
                    sp.dma_start(ea[:, s], ea_t[:, bass.ds(g, 1), :].rearrange("p a e -> p (a e)")).then_inc(ea_loaded[s], 16)
                    sp.dma_start(xrw[:, s], xr_tab[bass.ds(base, P)]).then_inc(ea_loaded[s], 16)
                if lo <= 3 < hi:
                    s = (j - 3) % UN
                    if not (isinstance(w, int) and w < UN + 3):
                        sp.wait_ge(v_y1, done(w, UN + 3))
                        alone(sp, sp_passed)
                    base = sp.value_load(item_i[0:1, 1, bass.ds(w - 3, 1)], min_val=0, max_val=N)
                    sp.dma_start(xw[:, s], x[bass.ds(base, P), :]).then_inc(xw_loaded[s], 16)
                if lo <= 6 < hi:
                    base = sp.value_load(item_i[0:1, 1, bass.ds(w - 6, 1)], min_val=0, max_val=N)
                    sp.wait_ge(a_out, done(w, 6))
                    alone(sp, sp_passed)
                    if not (isinstance(w, int) and w == 6):
                        sp.wait_ge(stored, (w - 6) * 16)
                        alone(sp, sp_passed)
                    sp.dma_start(out[bass.ds(base, P), :], ob[:, (j - 6) % 2]).then_inc(stored, 16)

            n_items = items(sp, step, 7)
            sp.wait_ge(stored, n_items * 16)
            alone(sp, sp_passed)

        @block.gpsimd
        def _(pool):
            nc.gpsimd.memset(ones[:], 1.0).then_inc(consts, 1)
            nc.gpsimd.iota(iota_w[:], pattern=[[1, WT]], base=0, channel_multiplier=0,
                           allow_small_or_imprecise_dtypes=True).then_inc(consts, 1)
            nc.gpsimd.iota(iota_p[:], pattern=[[0, 1]], base=0, channel_multiplier=1,
                           allow_small_or_imprecise_dtypes=True).then_inc(consts, 1)
            nc.gpsimd.iota(node_no[:], pattern=[[1, P], [0, CW]], base=0, channel_multiplier=0,
                           allow_small_or_imprecise_dtypes=True).then_inc(consts, 1)
            pool.wait_ge(consts, 4)
            nc.gpsimd.affine_select(out=tri[:], in_=ones[:], compare_op=ALU.is_ge, fill=0.0, base=0,
                                    pattern=[[1, P]], channel_multiplier=-1).then_inc(consts, 1)
            nc.gpsimd.affine_select(out=ident[:], in_=ones[:], compare_op=ALU.is_equal, fill=0.0, base=0,
                                    pattern=[[1, P]], channel_multiplier=-1).then_inc(consts, 1)

            def p_step(b, t, s, lo, hi):
                if lo <= 2 < hi:
                    k = (s - 2) % UP
                    pool.wait_ge(p_hi, b - 1)
                    nc.gpsimd.tensor_tensor(pres[:, k], pf[:, k, :, D:2 * D], pxr[:, k, :, 0], ALU.subtract).then_inc(p_res, 1)
                    pool.wait_ge(p_mid, b - 1)
                    nc.gpsimd.tensor_tensor(pxr[:, k, :, 2], pres[:, k], pxr[:, k, :, 1], ALU.subtract).then_inc(p_low, 1)

            batches(pool, p_step, 3)
            for s in range(UP):
                pool.wait_ge(p_stored[s], 32 * (BATCHES // UP))

            def gathers(w, j, r):
                pool.wait_ge(idx_loaded[j], in_slot(r, j, 0, UN, 32))
                if not (isinstance(w, int) and w < UN):
                    pool.wait_ge(v_msg, done(w, UN))
                alone(pool, pool_passed)
                for c in range(CH):
                    pool.indirect_dma_start(
                        out=gx[:, j, c, :], out_offset=None, in_=xl_tab,
                        in_offset=bass.IndirectOffsetOnAxis(ap=edg[:, j, 0, c:c + 1], axis=0),
                    ).then_inc(gathered[j], 16)

            items(pool, lambda w, j, r, lo, hi: gathers(w, j, r), 1)

        @block.tensor
        def _(pe):
            pe.wait_ge(consts, 6)
            pe.wait_ge(ptab, 1)
            pe.matmul(pch[:, 0:1], tri[:], bnd_f[:, 0:1], start=True, stop=True).then_inc(tab_ps, 1)
            pe.wait_ge(ptab, 2)
            pe.matmul(pch[:, 0:WT], ones[:], tabs[:, 0, :], start=True, stop=True).then_inc(tab_ps, 1)
            pe.matmul(pag[:, 0:WT], ones[:], tabs[:, 1, :], start=True, stop=True).then_inc(tab_ps, 1)
            pe.matmul(pnd[:, 0:WT], ones[:], tabs[:, 2, :], start=True, stop=True).then_inc(tab_ps, 1)
            pe.wait_ge(ptab, 3)
            pe.matmul(pch[:, 0:1], ones[:], bnd_f[:, 0:1], start=True, stop=True).then_inc(tab_ps, 1)

            pe.wait_ge(scaled, 3)
            pe.wait_ge(tables, 1)

            def p_step(b, t, s, lo, hi):
                if lo <= 1 < hi:
                    k = (s - 1) % UP
                    pe.wait_ge(p_hn, b)
                    if not (isinstance(b, int) and b < UP + 1):
                        pe.wait_ge(p_ht, b - UP)
                    for n in range(NB):
                        ins = pe.transpose(p_bank[k][:, n * P:(n + 1) * P], phn[:, k, n], ident[:])
                    ins.then_inc(p_tr, 1)
                    pe.wait_ge(p_ht, b)
                    if not (isinstance(b, int) and b < 2):
                        pe.wait_ge(p_add, b - 1)
                    for n in range(NB):
                        ins = pe.matmul(pz_rows[:, n], pht[:, k, n * P:(n + 1) * P], w_lr[:],
                                        start=n % 2 == 0, stop=n % 2 == 1 or n == NB - 1)
                    ins.then_inc(p_mm, 1)

            batches(pe, p_step, 2)

            def z_start(w, j, q):
                c0, n = GROUPS[q]
                if isinstance(w, int) and w == 1 and q < 2:
                    pe.wait_ge(p_add, BATCHES)
                else:
                    pe.wait_ge(v_leak, group(w, q - 2))
                for k in range(n):
                    pe.matmul(pz[:, q % 2, k], ea[:, (j - 1) % 2, (c0 + k) * P:(c0 + k + 1) * P], w_e[:], start=k == 0, stop=False)
                    if q not in SUMMED:
                        pe.matmul(pz[:, q % 2, k], ident[:], gx[:, (j - 1) % UN, c0 + k], start=False, stop=False)

            def z_end(w, j, q):
                c0, n = GROUPS[q]
                for k in range(n):
                    for part in range(3):
                        ins = pe.matmul(pz[:, q % 2, k], mt[:, (j - 1) % UN, (c0 + k) * P:(c0 + k + 1) * P],
                                        xrw[:, (j - 1) % 2, part], start=False, stop=k == n - 1 and part == 2)
                ins.then_inc(pe_z, 1)

            def sums(u):
                for k in range(CH):
                    ins = pe.matmul(aggr, m32[:, u, k], msg[:, k * H:(k + 1) * H].rearrange("p a b -> p (a b)"),
                                    start=k == 0, stop=k == CH - 1)
                ins.then_inc(pe_agg, 1)

            def step(w, j, r, lo, hi):
                p, a, b, c, d = (lo <= k < hi for k in range(5))
                v, u = (j - 2) % 2, (j - 3) % 2
                if a:
                    pe.wait_ge(ea_loaded[(j - 1) % 2], in_slot(r, j, 1, 2, 32))
                    pe.wait_ge(gathered[(j - 1) % UN], in_slot(r, j, 1, UN, 16 * CH))
                    z_start(w, j, 0)
                    pe.wait_ge(a_mt, done(w, 1, 2, 2))
                    z_end(w, j, 0)
                if d:
                    pe.wait_ge(a_hnt, done(w, 4))
                    for k in range(4):
                        ins = pe.matmul(pnd[:, k * P:(k + 1) * P], w_fc[:, k * P:(k + 1) * P], hnt[:],
                                        start=k == 0, stop=k == 3)
                    ins.then_inc(pe_fc, 1)
                if b:
                    pe.wait_ge(v_lg, done(w, 2, 2, 2))
                    pe.transpose(ch_lt[0:CH * H], lg[:, v, :], ident[:]).then_inc(pe_lt, 1)
                if a:
                    z_start(w, j, 1)
                    z_end(w, j, 1)
                if b:
                    pe.wait_ge(v_scan, done(w, 2))
                    pe.transpose(ch_vt, scan[0:CH * H, :], ident[0:CH * H, 0:CH * H]).then_inc(pe_vt, 1)
                if c:
                    pe.wait_ge(v_msg, done(w, 3))
                    pe.wait_ge(a_m32, done(w, 3))
                    sums(u)
                if b:
                    pe.wait_ge(v_low, done(w, 2))
                    pe.wait_ge(a_hi, done(w, 2))
                    for k in range(CH):
                        ins = pe.matmul(ch_cand[:, k], m16[:, (j - 2) % UN, :, k], vs[:, (j - 2) % UN, k],
                                        start=True, stop=True, skip_group_check=True)
                    ins.then_inc(pe_sel, 1)
                if a:
                    z_start(w, j, 2)
                    z_end(w, j, 2)
                if b:
                    if c:
                        pe.wait_ge(v_acc, done(w, 3))
                        pe.wait_ge(a_sel, done(w, 3))
                    pe.matmul(carry, sel[:, u], accs[:, u], start=True, stop=True).then_inc(pe_carry, 1)
                if a:
                    z_start(w, j, 3)
                    z_end(w, j, 3)
                if p:
                    pe.wait_ge(v_m, done(w, 0))
                    if not (isinstance(w, int) and w < 1):
                        pe.wait_ge(a_mt, done(w, 1, 2, 2))
                    for k in range(CH):
                        ins = pe.transpose(pmt[:, k // 8, (k % 8) * P:(k % 8 + 1) * P], m16[:, j, :, k], ident16[:])
                        if k in (7, CH - 1):
                            ins.then_inc(pe_mt, 1)
                if d:
                    pe.wait_ge(a_hid, done(w, 4))
                    if c:
                        pe.wait_ge(v_acc, done(w, 3))
                    else:
                        pe.wait_ge(v_y, done(w, 5))
                    for k in range(4):
                        ins = pe.matmul(mlp_out, hid[:, k], w_pr[:, k], start=k == 0, stop=k == 3)
                    ins.then_inc(pe_proj, 1)
                if c:
                    pe.wait_ge(a_hn, done(w, 3))
                    pe.transpose(pnd[:, 0:P], hn[:], ident[:]).then_inc(pe_ht, 1)
                if b:
                    pe.wait_ge(v_mlo, done(w, 2))
                    for k in range(CH):
                        ins = pe.matmul(ch_sh[:, k], mt[:, (j - 2) % UN, k * P:(k + 1) * P], ms[:],
                                        start=True, stop=True, skip_group_check=True)
                    ins.then_inc(pe_sh, 1)

            items(pe, step, 5)

        @block.scalar
        def _(act):
            nc.scalar.preload_act_table_set("natural_log_exp_and_others")
            act.wait_ge(tables, 1)

            def p_step(b, t, s, lo, hi):
                if lo <= 0 < hi:
                    act.wait_ge(p_stats, NB * b + NB)
                    if not (isinstance(b, int) and b < UP):
                        act.wait_ge(p_hn, b - (UP - 1))
                    nc.scalar.activation(plv[:, s], pmv[:, s, :, 1], ACT.Ln, bias=eps_t[:]).then_inc(p_ln, 1)
                    act.wait_ge(p_ln, b + 1)
                    nc.scalar.activation(prs[:, s], plv[:, s], ACT.Exp, scale=-0.5).then_inc(p_rstd, 1)
                if lo <= 1 < hi:
                    k = (s - 1) % UP
                    act.wait_ge(p_tr, b)
                    if not (isinstance(b, int) and b < UP + 1):
                        act.wait_ge(p_mm, b - UP)
                    nc.scalar.activation(pht[:, k], p_bank[k][:, 0:NB * P], ACT.Copy).then_inc(p_ht, 1)
                if lo <= 2 < hi:
                    k = (s - 2) % UP
                    act.wait_ge(p_add, b - 1)
                    if not (isinstance(b, int) and b < UP + 2):
                        act.wait_ge(p_stored[k], (t + (s - 2) // UP) * 32)
                    nc.scalar.activation(pxr[:, k, :, 0], pf[:, k, :, D:2 * D], ACT.Copy).then_inc(p_hi, 1)
                    act.wait_ge(p_res, b - 1)
                    nc.scalar.activation(pxr[:, k, :, 1], pres[:, k], ACT.Copy).then_inc(p_mid, 1)

            batches(act, p_step, 3)

            def relu(w, q):
                c0, n = GROUPS[q]
                if not (isinstance(w, int) and w < 2):
                    act.wait_ge(v_leak, group(w, q - 4))
                if q in SUMMED:
                    act.wait_ge(v_sum, done(w, 1, SUMMED.index(q) + 1, len(SUMMED)))
                else:
                    act.wait_ge(pe_z, group(w, q))
                nc.scalar.activation(zr[:, c0:c0 + n], zl[:, c0:c0 + n] if q in SUMMED else pz[:, q % 2, 0:n],
                                     ACT.Relu).then_inc(a_relu, 1)

            def one_hots(w, j, k):
                c0, m = HALVES[k]
                act.wait_ge(pe_mt, w * 2 + (k + 1))
                nc.scalar.activation(mt[:, j, c0 * P:(c0 + m) * P], pmt[:, k, 0:m * P], ACT.Copy).then_inc(a_mt, 1)

            def normalise(k, ready, at, rows, to, signal):
                act.wait_ge(*ready)
                nc.scalar.activation(neg2[:, k:k + 1], mv2[:, k, 0:1], ACT.Copy, scale=-1.0).then_inc(a_neg[k], 1)
                nc.scalar.activation(ln_v[:, k:k + 1], mv2[:, k, 1:2], ACT.Ln, bias=eps_t[:]).then_inc(a_ln[k], 1)
                act.wait_ge(a_ln[k], at)
                nc.scalar.activation(rs2[:, k:k + 1], ln_v[:, k:k + 1], ACT.Exp, scale=-0.5).then_inc(a_rs[k], 1)
                act.wait_ge(a_neg[k], at)
                act.wait_ge(a_rs[k], at)
                nc.scalar.activation(off2[:, k:k + 1], neg2[:, k:k + 1], ACT.Identity, scale=rs2[:, k:k + 1]).then_inc(a_off[k], 1)
                act.wait_ge(a_off[k], at)
                nc.scalar.activation(to, rows, ACT.Identity, scale=rs2[:, k:k + 1], bias=off2[:, k:k + 1]).then_inc(signal, 1)

            def step(w, j, r, lo, hi):
                p, a, b, c, d = (lo <= k < hi for k in range(5))
                n, i, v, u, y = j % 2, (j - 1) % 2, (j - 2) % 2, (j - 3) % 2, (j - 4) % 2
                if a:
                    relu(w, 0)
                if d:
                    act.wait_ge(pe_fc, done(w, 4))
                    nc.scalar.activation(hid[:].rearrange("p a n -> p (a n)"), pnd[:], ACT.Relu).then_inc(a_hid, 1)
                if a:
                    relu(w, 1)
                if p:
                    act.wait_ge(idx_loaded[j], in_slot(r, j, 0, UN, 32))
                    nc.scalar.activation(dl[:, n], edg[:, j, 1], ACT.Identity, bias=minus_base[:, bass.ds(w, 1)]).then_inc(a_dl, 1)
                if b:
                    act.wait_ge(v_vlast, done(w, 2))
                    nc.scalar.activation(vs[:, (j - 2) % UN, :, 0:H], vlast[:], ACT.Copy).then_inc(a_hi, 1)
                if c:
                    nc.scalar.activation(apart[:], iota_p[:], ACT.Square, bias=minus_delta[:, bass.ds(w - 3, 1)]).then_inc(a_apart, 1)
                    act.wait_ge(a_apart, done(w, 3))
                    nc.scalar.activation(sel[:, u, 0:1], apart[:], ACT.Relu, scale=-1.0, bias=ones[:, 0:1]).then_inc(a_sel, 1)
                if a:
                    act.wait_ge(v_m, done(w, 1))
                    if c:
                        act.wait_ge(pe_agg, done(w, 3))
                    nc.scalar.activation(m32[:, i], m16[:, (j - 1) % UN].rearrange("p n c -> p c n")[:, 0:CH], ACT.Copy).then_inc(a_m32, 1)
                    relu(w, 2)
                if p:
                    act.wait_ge(v_diff, done(w, 0))
                    nc.scalar.activation(runf[0:CH * H, n], runf[0:CH * H, n], ACT.Copy, scale=BIG).then_inc(a_runf, 1)
                if c:
                    normalise(0, (v_mv, done(w, 3)), done(w, 3), x1[:, u], hn[:], a_hn)
                if p:
                    one_hots(w, j, 0)
                if a:
                    relu(w, 3)
                if p:
                    one_hots(w, j, 1)
                if b:
                    act.wait_ge(v_farg, done(w, 2))
                    nc.scalar.activation(fac[:, v], farg[:], ACT.Exp).then_inc(a_fac, 1)
                if c:
                    act.wait_ge(pe_ht, done(w, 3))
                    nc.scalar.activation(hnt[:], pnd[:, 0:P], ACT.Copy).then_inc(a_hnt, 1)
                if b:
                    act.wait_ge(v_dmin, done(w, 2))
                    if c:
                        act.wait_ge(pe_agg, done(w, 3))
                    nc.scalar.activation(msg[:, :, HC], dmin[:], ACT.Exp).then_inc(a_exp, 1)
                if d:
                    if not (isinstance(w, int) and w < 6):
                        act.wait_ge(stored, (w - 5) * 16)
                    normalise(1, (v_mvf, done(w, 4)), done(w, 4), y1[:, y], ob[:, y], a_out)

            items(act, step, 5)

        @block.vector
        def _(dve):
            V = nc.vector
            dve.wait_ge(bounds_loaded, 16)
            t = [0]

            def link(ins):
                t[0] += 1
                ins.then_inc(table_steps, 1)
                dve.wait_ge(table_steps, t[0])

            link(V.tensor_tensor(bnd_d[:], bnd[:, 1:2], bnd[:, 0:1], ALU.subtract))
            link(V.tensor_scalar(bnd_d[:], bnd_d[:], 7, None, ALU.arith_shift_right))
            V.tensor_scalar(bnd_f[:, 0:1], bnd_d[:], 1.0, None, ALU.add).then_inc(ptab, 1)
            dve.wait_ge(tab_ps, 1)
            link(V.tensor_copy(bnd_f[:, 1:2], pch[:, 0:1]))
            link(V.tensor_tensor(bnd_f[:, 2:3], bnd_f[:, 1:2], bnd_f[:, 0:1], ALU.subtract))
            link(V.tensor_copy(bnd_f[:, 3:4], bnd[:, 0:1]))
            link(V.scalar_tensor_tensor(bnd_f[:, 4:5], bnd_f[:, 2:3], -float(P), bnd_f[:, 3:4], ALU.mult, ALU.add))
            dve.wait_ge(consts, 6)
            link(V.tensor_scalar(tabs[:, 3, :], iota_w[:], bnd_f[:, 2:3], None, ALU.is_ge))
            link(V.scalar_tensor_tensor(tabs[:, 1, :], iota_w[:], bnd_f[:, 1:2], tabs[:, 3, :], ALU.is_lt, ALU.mult))
            link(V.tensor_scalar(tabs[:, 3, :], iota_w[:], float(P), bnd_f[:, 4:5], ALU.mult, ALU.add))
            link(V.tensor_tensor(tabs[:, 0, :], tabs[:, 3, :], tabs[:, 1, :], ALU.mult))
            V.tensor_scalar(tabs[:, 2, :], iota_w[:], bnd_f[:, 1:2], None, ALU.is_ge).then_inc(ptab, 1)
            dve.wait_ge(tab_ps, 4)
            link(V.tensor_scalar(tabs[:, 3, :], pag[:, 0:WT], -float(N), float(N), ALU.mult, ALU.add))
            link(V.tensor_tensor(base_f[:], tabs[:, 3, :], pch[:, 0:WT], ALU.add))
            link(V.tensor_scalar(item_i[:, 0, :], pnd[:, 0:WT], float(G - 1), None, ALU.min))
            link(V.tensor_copy(item_i[:, 1, :], base_f[:]))
            link(V.tensor_scalar(minus_base[:], base_f[:], -1.0, None, ALU.mult))
            link(V.memset(minus_delta[:], 0.0))
            V.tensor_tensor(minus_delta[:, 0:WT - 1], base_f[:, 0:WT - 1], base_f[:, 1:WT], ALU.subtract).then_inc(ptab, 1)
            dve.wait_ge(tab_ps, 5)
            link(V.tensor_copy(bnd_f[:, 5:6], pch[:, 0:1]))
            link(V.tensor_scalar(cnt_f[:, 0, :], iota_w[:, 0:P], float(UN), bnd_f[:, 5:6], ALU.mult, ALU.is_lt))
            link(V.tensor_reduce(bnd_f[:, 6:7], cnt_f[:, 0, :], AX.X, ALU.add))
            link(V.tensor_scalar(more_i[:], bnd_f[:, 6:7], float(-(G // UN)), None, ALU.add))
            dve.wait_ge(w_loaded, 16 * LOADS)
            V.tensor_scalar(w_lr[:], w_lr[:], ln1[:], None, ALU.mult).then_inc(scaled, 1)
            V.tensor_scalar(w_fc[:], w_fc[:], ln2[:], None, ALU.mult).then_inc(scaled, 1)
            V.tensor_copy(ident16[:], ident[:]).then_inc(scaled, 1)
            link(V.tensor_scalar(att_b[:], att_b[:], 1.0 - SLOPE, None, ALU.mult))
            link(V.memset(sel[:], 0.0))
            link(V.memset(accs[:], 0.0))
            link(V.memset(accs[:, :, AW + H:AW + H + 1], 1.0))
            link(V.memset(runf[:], 0.0))
            link(V.memset(vs[:], 0.0))
            V.memset(eps_t[:], EPS).then_inc(tables, 1)
            dve.wait_ge(tables, 1)

            def p_step(b, t, s, lo, hi):
                if lo <= 1 < hi:
                    k = (s - 1) % UP
                    dve.wait_ge(p_rstd, b)
                    if not (isinstance(b, int) and b < UP + 1):
                        dve.wait_ge(p_tr, b - UP)
                    for n in range(NB):
                        ins = V.tensor_scalar(phn[:, k, n], px[:, k, n], pmv[:, k, n, 0:1], prs[:, k, n:n + 1],
                                              ALU.subtract, ALU.mult)
                    ins.then_inc(p_hn, 1)
                if lo <= 0 < hi:
                    dve.wait_ge(px_loaded[s], 16 * t + 16)
                    for n in range(NB):
                        ins = V.bn_stats(pst[:, s, n], px[:, s, n])
                    ins.then_inc(p_bn, 1)
                    dve.wait_ge(p_bn, b + 1)
                    alone(dve, dve_passed)
                    for n in range(NB):
                        V.bn_aggr(pmv[:, s, n], pst[:, s, n]).then_inc(p_stats, 1)
                if lo <= 2 < hi:
                    k = (s - 2) % UP
                    if not (isinstance(b, int) and b < UP + 2):
                        dve.wait_ge(p_stored[k], (t + (s - 2) // UP) * 32)
                    dve.wait_ge(p_mm, b - 1)
                    V.tensor_tensor(pf[:, k], pz_rows[:, 0:NB], b_lr[:].unsqueeze(1).broadcast_to([P, NB, 2 * D]),
                                    ALU.add).then_inc(p_add, 1)

            batches(dve, p_step, 3)

            def add_xl(w, j, q):
                c0, n = GROUPS[q]
                dve.wait_ge(pe_z, group(w, q))
                V.tensor_tensor(zl[:, c0:c0 + n], pz[:, q % 2, 0:n], gx[:, (j - 1) % UN, c0:c0 + n], ALU.add).then_inc(v_sum, 1)

            def leaky(w, q):
                c0, n = GROUPS[q]
                dve.wait_ge(a_relu, group(w, q))
                V.scalar_tensor_tensor(zl[:, c0:c0 + n], zl[:, c0:c0 + n] if q in SUMMED else pz[:, q % 2, 0:n],
                                       SLOPE / (1.0 - SLOPE), zr[:, c0:c0 + n],
                                       ALU.mult, ALU.add).then_inc(v_leak, 1)

            def times_att(w, q):
                c0, n = GROUPS[q]
                dve.wait_ge(v_leak, group(w, q))
                V.tensor_tensor(zl[:, c0:c0 + n], zl[:, c0:c0 + n], att_b[:].unsqueeze(1).broadcast_to([P, n, D]),
                                ALU.mult).then_inc(v_att, 1)

            def logits(w, j, half):
                c0, n = HALVES[half]
                dve.wait_ge(v_att, group(w, 2 * half + 1))
                V.tensor_reduce(lg[:, (j - 1) % 2, c0 * H:(c0 + n) * H],
                                zl[:, c0:c0 + n].rearrange("p c (h k) -> p (c h) k", k=HC), AX.X, ALU.add).then_inc(v_lg, 1)

            def step(w, j, r, lo, hi):
                p, a, b, c, d = (lo <= k < hi for k in range(5))
                n, v, u, y = j % 2, (j - 2) % 2, (j - 3) % 2, (j - 4) % 2
                xu = (j - 3) % UN
                if b:
                    dve.wait_ge(pe_lt, done(w, 2))
                    dve.wait_ge(a_runf, done(w, 2))
                    V.tensor_tensor_scan(scan[0:CH * H, :], runf[0:CH * H, v], ch_lt[0:CH * H], -BIG,
                                         ALU.add, ALU.max).then_inc(v_scan, 1)
                if a:
                    leaky(w, 0)
                if c:
                    dve.wait_ge(xw_loaded[xu], in_slot(r, j, 3, UN, 16))
                    V.tensor_tensor(xab[:], xw[:, xu], a_bias[:], ALU.add)
                if a:
                    times_att(w, 0)
                if b:
                    dve.wait_ge(pe_vt, done(w, 2))
                    V.tensor_tensor(vlast[:], ch_vt.rearrange("p (c h) -> p c h", h=H),
                                    vs[:, (j - 2) % UN, :, H:H + 1].broadcast_to([P, CH, H]), ALU.mult).then_inc(v_vlast, 1)
                if a:
                    leaky(w, 1)
                if b:
                    dve.wait_ge(a_hi, done(w, 2))
                    V.tensor_tensor(vs[:, (j - 2) % UN, :, H + 1:2 * H + 1], vlast[:], vs[:, (j - 2) % UN, :, 0:H],
                                    ALU.subtract).then_inc(v_low, 1)
                if a:
                    times_att(w, 1)
                if p:
                    dve.wait_ge(a_dl, done(w, 0))
                    V.tensor_tensor(m16[:, j], dl[:, n].unsqueeze(1).broadcast_to([P, P, CW]), node_no[:],
                                    ALU.is_equal).then_inc(v_m, 1)
                if c:
                    dve.wait_ge(pe_agg, done(w, 3))
                    dve.wait_ge(v_tmp, done(w, 3))
                    V.tensor_tensor(accs[:, u, 0:AW], tmpa[:], aggr, ALU.add).then_inc(v_acc, 1)
                if p:
                    dve.wait_ge(idx_loaded[j], in_slot(r, j, 0, UN, 32))
                    V.tensor_tensor(vs[:, j, :, H], edg[:, j, 1, 0:CH], edg[:, j, 2, 0:CH], ALU.not_equal).then_inc(v_last, 1)
                if c:
                    dve.wait_ge(v_acc, done(w, 3))
                    V.tensor_scalar(rden[:, 0], accs[:, u, HC:AW:MS], 1e-30, None, ALU.max).then_inc(v_den, 1)
                if p:
                    V.tensor_tensor(runf[0:CH * H, n, 1:P], drow[0:CH * H, j, 0:P - 1], drow[0:CH * H, j, 1:P],
                                    ALU.subtract).then_inc(v_diff, 1)
                if c:
                    dve.wait_ge(v_den, done(w, 3))
                    V.reciprocal(rden[:, 1], rden[:, 0]).then_inc(v_rden, 1)
                if b:
                    dve.wait_ge(pe_sel, done(w, 2))
                    V.tensor_scalar(pen[:], ch_cand[:, :, H], -1.0, BIG, ALU.add, ALU.mult).then_inc(v_pen, 1)
                if c:
                    dve.wait_ge(v_rden, done(w, 3))
                    V.tensor_tensor(attn[:].rearrange("p (h k) -> p h k", k=HC),
                                    accs[:, u, 0:AW].rearrange("p (h k) -> p h k", k=MS)[:, :, 0:HC],
                                    rden[:, 1].unsqueeze(2).broadcast_to([P, H, HC]), ALU.mult).then_inc(v_attn, 1)
                if b:
                    dve.wait_ge(v_pen, done(w, 2))
                    V.tensor_tensor(cand_low[:], ch_cand[:, :, H + 1:2 * H + 1],
                                    pen[:].unsqueeze(2).broadcast_to([P, CH, H]), ALU.add).then_inc(v_clow, 1)
                if c:
                    dve.wait_ge(v_attn, done(w, 3))
                    V.tensor_tensor(x1[:, u], attn[:], xab[:], ALU.add).then_inc(v_x1, 1)
                if b:
                    dve.wait_ge(v_clow, done(w, 2))
                    V.tensor_tensor(cand[:], ch_cand[:, :, 0:H], cand_low[:], ALU.add).then_inc(v_cand, 1)
                if c:
                    dve.wait_ge(v_x1, done(w, 3))
                    V.bn_stats(st2[:, 0], x1[:, u]).then_inc(v_st, 1)
                if a:
                    leaky(w, 2)
                if c:
                    dve.wait_ge(v_st, done(w, 3))
                    alone(dve, dve_passed)
                    V.bn_aggr(mv2[:, 0], st2[:, 0]).then_inc(v_mv, 1)
                if b:
                    dve.wait_ge(v_cand, done(w, 2))
                    V.tensor_reduce(mblk[:], cand[:].rearrange("p c h -> p h c"), AX.X, ALU.max).then_inc(v_mblk, 1)
                    dve.wait_ge(pe_carry, done(w, 2))
                    V.tensor_scalar(pen2[:], carry[:, AW + H:AW + H + 1], -1.0, BIG, ALU.add, ALU.mult).then_inc(v_pen2, 1)
                if a:
                    times_att(w, 2)
                if b:
                    dve.wait_ge(v_mblk, done(w, 2))
                    dve.wait_ge(v_pen2, done(w, 2))
                    V.scalar_tensor_tensor(accs[:, v, AW:AW + H], carry[:, AW:AW + H], pen2[:], mblk[:],
                                           ALU.add, ALU.max).then_inc(v_max, 1)
                if c:
                    if not (isinstance(w, int) and w < 5):
                        dve.wait_ge(a_out, done(w, 5))
                    V.tensor_tensor(y1[:, u], x1[:, u], xw[:, xu], ALU.add).then_inc(v_y1, 1)
                if b:
                    dve.wait_ge(v_max, done(w, 2))
                    V.tensor_copy(ms[:, 0:H], accs[:, v, AW:AW + H]).then_inc(v_mhi, 1)
                    V.scalar_tensor_tensor(farg[:], carry[:, AW:AW + H], pen2[:], accs[:, v, AW:AW + H],
                                           ALU.add, ALU.subtract).then_inc(v_farg, 1)
                    dve.wait_ge(v_mhi, done(w, 2))
                    V.tensor_tensor(ms[:, H:2 * H], accs[:, v, AW:AW + H], ms[:, 0:H], ALU.subtract).then_inc(v_mlo, 1)
                if a:
                    add_xl(w, j, 3)
                    logits(w, j, 0)
                if d:
                    if not c:
                        dve.wait_ge(a_out, done(w, 5))
                    dve.wait_ge(v_y1, done(w, 4))
                    dve.wait_ge(pe_proj, done(w, 4))
                    V.tensor_tensor(y1[:, y], y1[:, y], mlp_out, ALU.add).then_inc(v_y, 1)
                if b:
                    dve.wait_ge(pe_sh, done(w, 2))
                    V.tensor_tensor(dlt_hi[:], lg[:, v].rearrange("p (c h) -> p c h", h=H), ch_sh[:, :, 0:H],
                                    ALU.subtract).then_inc(v_dhi, 1)
                if d:
                    dve.wait_ge(v_y, done(w, 4))
                    V.bn_stats(st2[:, 1], y1[:, y]).then_inc(v_stf, 1)
                if b:
                    dve.wait_ge(v_dhi, done(w, 2))
                    V.tensor_tensor(dlt[:].rearrange("p (c h) -> p c h", h=H), dlt_hi[:], ch_sh[:, :, H:2 * H],
                                    ALU.subtract).then_inc(v_dlt, 1)
                if a:
                    leaky(w, 3)
                if b:
                    dve.wait_ge(v_dlt, done(w, 2))
                    V.tensor_scalar(dmin[:], dlt[:], 0.0, None, ALU.min).then_inc(v_dmin, 1)
                if d:
                    dve.wait_ge(v_stf, done(w, 4))
                    alone(dve, dve_passed)
                    V.bn_aggr(mv2[:, 1], st2[:, 1]).then_inc(v_mvf, 1)
                if a:
                    times_att(w, 3)
                if b:
                    dve.wait_ge(a_fac, done(w, 2))
                    V.tensor_tensor(tmpa[:].rearrange("p (h k) -> p h k", k=MS),
                                    carry[:, 0:AW].rearrange("p (h k) -> p h k", k=MS),
                                    fac[:, v].unsqueeze(2).broadcast_to([P, H, MS]), ALU.mult).then_inc(v_tmp, 1)
                if a:
                    logits(w, j, 1)
                if b:
                    dve.wait_ge(a_exp, done(w, 2))
                    V.tensor_tensor(msg[:, :, 0:HC], gx[:, (j - 2) % UN].rearrange("p c (h k) -> p (c h) k", k=HC),
                                    msg[:, :, HC:MS].broadcast_to([P, CH * H, HC]), ALU.mult).then_inc(v_msg, 1)

            items(dve, step, 5)


def kernel(x, src, dst, edge_attr_128, L0_gnn_ln1_w, L0_gnn_lin_l_w, L0_gnn_lin_l_b, L0_gnn_lin_r_w,
           L0_gnn_lin_r_b, L0_gnn_lin_edge_w, L0_gnn_att, L0_gnn_attn_bias, L0_gnn_ln2_w, L0_gnn_fc_w,
           L0_gnn_proj_w):
    import numpy as np
    import concourse.bacc as bacc
    from concourse.bass_utils import run_bass_kernel_spmd

    a = lambda v: np.asarray(v)
    xs = np.zeros((NP, D), np.float32)
    xs[:N] = a(x)
    ea_t = np.zeros((D, EP), np.float32)
    ea_t[:, :E] = a(edge_attr_128).T
    src_p, dst_p = np.zeros(EP, np.int32), np.full(EP, -1, np.int32)
    src_p[:E], dst_p[:E] = a(src), a(dst)
    edges = np.full((P, G, 3, CW), -1, np.int32)
    edges[:, :, 0, :CH] = src_p.reshape(G, CH, P).transpose(2, 0, 1)
    edges[:, :, 0, CH:] = 0
    edges[:, :, 1, :CH] = dst_p.reshape(G, CH, P).transpose(2, 0, 1)
    edges[:-1, :, 2, :CH] = edges[1:, :, 1, :CH]
    edges[-1, :, 2, :] = -2
    dst_row = np.repeat(dst_p.reshape(G, CH, P), H, axis=1)
    bounds = np.zeros((P, 2), np.int32)
    bounds[:, 1] = -P
    ends = dst_p[EG - 1:E:EG][:G - 1]
    bounds[1:G, 0] = ends
    bounds[:G - 1, 1] = ends
    bounds[G - 1, 1] = N - 1
    arrays = {
        "x": xs,
        "ea_t": ea_t.reshape(D, G, EG),
        "edges": edges,
        "dst_row": dst_row,
        "bounds": bounds,
        "ln1_w": a(L0_gnn_ln1_w).reshape(D, 1),
        "wlr_t": np.concatenate([a(L0_gnn_lin_l_w).T, a(L0_gnn_lin_r_w).T], 1),
        "blr": np.concatenate([a(L0_gnn_lin_l_b), a(L0_gnn_lin_r_b)]).reshape(1, 2 * D),
        "we_t": a(L0_gnn_lin_edge_w).T,
        "att": a(L0_gnn_att).reshape(1, D),
        "attn_bias": a(L0_gnn_attn_bias).reshape(1, D),
        "ln2_w": a(L0_gnn_ln2_w).reshape(D, 1),
        "fc_t": a(L0_gnn_fc_w).T,
        "proj_t": a(L0_gnn_proj_w).T.reshape(4, P, D).transpose(1, 0, 2),
    }
    arrays = {k: np.ascontiguousarray(v) for k, v in arrays.items()}
    nc = bacc.Bacc("TRN2", target_bir_lowering=False, num_devices=1)
    args = {k: nc.dram_tensor(f"{k}_in", v.shape, mybir.dt.from_np(v.dtype), kind="ExternalInput").ap()
            for k, v in arrays.items()}
    out = nc.dram_tensor("out_rows", (NP, D), F32, kind="ExternalOutput").ap()
    gnn_kernel(nc, out=out, **args)
    r = run_bass_kernel_spmd(nc, [{f"{k}_in": v for k, v in arrays.items()}], core_ids=[0])
    return r.results[0]["out_rows"][:N]
```
